# Optimizing a Trainium2 kernel written in Bass

```python
import numpy as np
import jax
import jax.numpy as jnp

def _softmax(x, axis=-1):
    return jax.nn.softmax(x, axis=axis)

def _gelu(x):
    return jax.nn.gelu(x, approximate=True)

def _silu(x):
    return jax.nn.silu(x)

def _sigmoid(x):
    return jax.nn.sigmoid(x)

def _layernorm(x, axis=-1, eps=1e-05):
    m = jnp.mean(x, axis=axis, keepdims=True)
    v = jnp.var(x, axis=axis, keepdims=True)
    return (x - m) / jnp.sqrt(v + eps)

def _scatter_add(tgt, idx, src, axis=0):
    return tgt.at[idx].add(src)

def _segment_sum(src, seg, n):
    return jax.ops.segment_sum(src, seg, n)
kernel_name = 'mk_decoder_postln_d2_seqx_r8_c6d31b'

def setup_inputs(seed: int=0):
    np.random.seed(seed)
    _w = jnp.asarray

    def _rec_inputs():
        import jax
        import jax.numpy as jnp
        _rk = jax.random.key(seed)
        x = -1.394e-06 + 0.9999 * jax.random.normal(jax.random.fold_in(_rk, 1), (64, 64, 128), jnp.float32)
        _lenS = 64 - jax.random.randint(jax.random.fold_in(_rk, 7), (64,), 0, max(1, 64 // 4) + 1, jnp.int32)
        _lenS2 = 64 - jax.random.randint(jax.random.fold_in(_rk, 8), (64,), 0, max(1, 64 // 4) + 1, jnp.int32)
        _ctx_1024P = jax.random.normal(jax.random.fold_in(_rk, 11), (64, 16, 128), jnp.float32)
        _ctx_1024c = jax.random.dirichlet(jax.random.fold_in(_rk, 511), 0.3 * jnp.ones((16,), jnp.float32), (64, 64))
        _ctx_1024t = jnp.einsum('bsk,bkd->bsd', _ctx_1024c, _ctx_1024P)
        _ctx_1024t = _ctx_1024t * jax.lax.rsqrt(jnp.mean(jnp.square(_ctx_1024t)) + 1e-12) * 0.953939
        ctx_1024 = 7.22013e-05 + 1.00017 * (_ctx_1024t + 0.3 * jax.random.normal(jax.random.fold_in(_rk, 611), (64, 64, 128), jnp.float32))
        _validS = jnp.arange(64)[None, :] < _lenS[:, None]
        _validS2 = jnp.arange(64)[None, :] < _lenS2[:, None]
        _causal = jnp.tril(jnp.ones((64, 64), dtype=bool))
        mask_BxSxS2_ik0 = jnp.where(jnp.broadcast_to(_validS2[:, None, :], (64, 64, 64)), 0, 1).astype(jnp.int32)
        return (x, ctx_1024, mask_BxSxS2_ik0)
    x, ctx_1024, mask_BxSxS2_ik0 = _rec_inputs()

    def _L0_attn_setup():
        import jax, jax.numpy as jnp
        import numpy as np
        B, N, D = (2, 256, 128)
        H, DK, DV = (8, 128, 128)
        key = jax.random.key(seed)
        kx, kq, kk, kv = jax.random.split(key, 4)
        scale = 0.02
        x = jax.random.normal(kx, (B, N, D), dtype=jnp.float32)
        Wq = jax.random.normal(kq, (H, DK, D), dtype=jnp.float32) * scale
        Wk = jax.random.normal(kk, (H, DK, D), dtype=jnp.float32) * scale
        Wv = jax.random.normal(kv, (H, DV, D), dtype=jnp.float32) * scale
        return {'x': x, 'Wq': Wq, 'Wk': Wk, 'Wv': Wv}
    _L0_attn_all = _L0_attn_setup()
    _L0_attn_in = {k: v for k, v in _L0_attn_all.items() if k in ('Wq', 'Wk', 'Wv')}
    del _L0_attn_all

    def _L0_xattn_setup():
        import jax, jax.numpy as jnp
        import numpy as np
        B, NKV, NQ, D, H = (4, 256, 128, 128, 16)
        HD = D // H
        key = jax.random.key(seed)
        ks = jax.random.split(key, 9)
        s = 0.02
        return {'x': jax.random.normal(ks[0], (B, NKV, D), jnp.float32), 'y': jax.random.normal(ks[1], (B, NQ, D), jnp.float32), 'mask': jax.random.randint(ks[2], (B, NQ, NKV), 0, 2, jnp.int32), 'W_kv': jax.random.normal(ks[3], (D, 2 * D), jnp.float32) * s, 'b_kv': jnp.zeros((2 * D,), jnp.float32), 'W_q': jax.random.normal(ks[4], (D, D), jnp.float32) * s, 'b_q': jnp.zeros((D,), jnp.float32), 'W_o': jax.random.normal(ks[5], (D, D), jnp.float32) * s, 'b_o': jnp.zeros((D,), jnp.float32)}
    _L0_xattn_all = _L0_xattn_setup()
    _L0_xattn_in = {k: v for k, v in _L0_xattn_all.items() if k in ('W_kv', 'b_kv', 'W_q', 'b_q', 'W_o', 'b_o')}
    del _L0_xattn_all

    def _L0_ffn_setup():
        import jax, jax.numpy as jnp
        import numpy as np
        D_MODEL = 128
        MLP_DIM = 512
        N_EXPERTS = 8
        B, T = (4, 128)
        key = jax.random.key(seed)
        ks = jax.random.split(key, 7)
        scale_in = (1.0 / D_MODEL) ** 0.5
        scale_out = (1.0 / MLP_DIM) ** 0.5
        bound_g = (1.0 / D_MODEL) ** 0.5
        w_gate = jax.random.uniform(ks[0], (D_MODEL, N_EXPERTS), minval=-bound_g, maxval=bound_g, dtype=jnp.float32)
        b_gate = jax.random.uniform(ks[1], (N_EXPERTS,), minval=-bound_g, maxval=bound_g, dtype=jnp.float32)
        W1 = jax.random.uniform(ks[2], (N_EXPERTS, D_MODEL, MLP_DIM), minval=-scale_in, maxval=scale_in, dtype=jnp.float32)
        b1 = jnp.zeros((N_EXPERTS, MLP_DIM), dtype=jnp.float32)
        W2 = jax.random.uniform(ks[3], (N_EXPERTS, MLP_DIM, D_MODEL), minval=-scale_out, maxval=scale_out, dtype=jnp.float32)
        b2 = jnp.zeros((N_EXPERTS, D_MODEL), dtype=jnp.float32)
        x = jax.random.normal(ks[4], (B, T, D_MODEL), dtype=jnp.float32)
        return {'x': x, 'w_gate': w_gate, 'b_gate': b_gate, 'W1': W1, 'b1': b1, 'W2': W2, 'b2': b2}
    _L0_ffn_all = _L0_ffn_setup()
    _L0_ffn_in = {k: v for k, v in _L0_ffn_all.items() if k in ('w_gate', 'b_gate', 'W1', 'b1', 'W2', 'b2')}
    del _L0_ffn_all

    def _L1_attn_setup():
        import jax, jax.numpy as jnp
        import numpy as np
        DECAY = 0.99
        LR = 0.01

        def _reference_tuple_inner(x, Wk, bk, Wv, bv, Wq, bq, Wo, bo):
            B, S, D = x.shape
            M = Wk.shape[0]
            k = jnp.einsum('bsd,md->bsm', x, Wk) + bk
            v = jnp.einsum('bsd,md->bsm', x, Wv) + bv
            q = jnp.einsum('bsd,md->bsm', x, Wq) + bq

            def step(state, kvq):
                k_t, v_t, q_t = kvq
                out_t = jnp.einsum('bij,bj->bi', state, q_t)
                state = DECAY * state + LR * jnp.einsum('bi,bj->bij', v_t, k_t)
                return (state, out_t)
            state0 = jnp.zeros((B, M, M), x.dtype)
            xs = (jnp.swapaxes(k, 0, 1), jnp.swapaxes(v, 0, 1), jnp.swapaxes(q, 0, 1))
            state, outs = jax.lax.scan(step, state0, xs)
            outs = jnp.swapaxes(outs, 0, 1)
            y = jnp.einsum('bsm,dm->bsd', outs, Wo) + bo
            return (y, state)
        key = jax.random.key(seed)
        ks = jax.random.split(key, 6)
        B, S, D, M = (4, 512, 128, 128)
        sD = 1.0 / np.sqrt(D)
        sM = 1.0 / np.sqrt(M)
        return {'x': jax.random.normal(ks[0], (B, S, D), dtype=jnp.float32), 'Wk': jax.random.uniform(ks[1], (M, D), jnp.float32, -sD, sD), 'bk': jnp.zeros((M,), jnp.float32), 'Wv': jax.random.uniform(ks[2], (M, D), jnp.float32, -sD, sD), 'bv': jnp.zeros((M,), jnp.float32), 'Wq': jax.random.uniform(ks[3], (M, D), jnp.float32, -sD, sD), 'bq': jnp.zeros((M,), jnp.float32), 'Wo': jax.random.uniform(ks[4], (D, M), jnp.float32, -sM, sM), 'bo': jnp.zeros((D,), jnp.float32)}
    _L1_attn_all = _L1_attn_setup()
    _L1_attn_in = {k: v for k, v in _L1_attn_all.items() if k in ('Wk', 'bk', 'Wv', 'bv', 'Wq', 'bq', 'Wo', 'bo')}
    del _L1_attn_all

    def _L1_xattn_setup():
        import jax, jax.numpy as jnp
        import numpy as np
        B, KV_LEN, Q_LEN = (8, 256, 64)
        D, H = (128, 16)
        HD = D // H
        key = jax.random.key(seed)
        ks = jax.random.split(key, 8)
        s = 1.0 / np.sqrt(D)
        return {'KV': jax.random.normal(ks[0], (B, KV_LEN, D), jnp.float32), 'Q': jax.random.normal(ks[1], (B, Q_LEN, D), jnp.float32), 'Wq': jax.random.normal(ks[2], (D, D), jnp.float32) * s, 'bq': jnp.zeros((D,), jnp.float32), 'Wk': jax.random.normal(ks[3], (D, D), jnp.float32) * s, 'bk': jnp.zeros((D,), jnp.float32), 'Wo': jax.random.normal(ks[4], (D, D), jnp.float32) * s, 'bo': jnp.zeros((D,), jnp.float32)}
    _L1_xattn_all = _L1_xattn_setup()
    _L1_xattn_in = {k: v for k, v in _L1_xattn_all.items() if k in ('Wq', 'bq', 'Wk', 'bk', 'Wo', 'bo')}
    del _L1_xattn_all

    def _L1_ffn_setup():
        import jax, jax.numpy as jnp
        import numpy as np
        D_MODEL = 128
        EXPERT_DIM = 64
        N_EXPERTS = 8
        TOP_K = 2

        def _sq_relu(h):
            return jnp.square(jax.nn.relu(h))
        key = jax.random.key(seed)
        ks = jax.random.split(key, 6)
        s = 0.02
        x = jax.random.normal(ks[0], (2, 256, D_MODEL), dtype=jnp.float32)
        Ws1 = jax.random.normal(ks[1], (D_MODEL, EXPERT_DIM), dtype=jnp.float32) * s
        Ws2 = jax.random.normal(ks[2], (EXPERT_DIM, D_MODEL), dtype=jnp.float32) * s
        W1 = jax.random.normal(ks[3], (N_EXPERTS, D_MODEL, EXPERT_DIM), dtype=jnp.float32) * s
        W2 = jax.random.normal(ks[4], (N_EXPERTS, EXPERT_DIM, D_MODEL), dtype=jnp.float32) * s
        Wr = jax.random.normal(ks[5], (D_MODEL, N_EXPERTS), dtype=jnp.float32) * s
        return {'x': x, 'Ws1': Ws1, 'Ws2': Ws2, 'W1': W1, 'W2': W2, 'Wr': Wr}
    _L1_ffn_all = _L1_ffn_setup()
    _L1_ffn_in = {k: v for k, v in _L1_ffn_all.items() if k in ('Ws1', 'Ws2', 'W1', 'W2', 'Wr')}
    del _L1_ffn_all
    return {'x': x, 'ctx_1024': ctx_1024, 'mask_BxSxS2_ik0': mask_BxSxS2_ik0, 'L0_attn_Wq': _L0_attn_in['Wq'], 'L0_attn_Wk': _L0_attn_in['Wk'], 'L0_attn_Wv': _L0_attn_in['Wv'], 'L0_xattn_W_kv': _L0_xattn_in['W_kv'], 'L0_xattn_b_kv': _L0_xattn_in['b_kv'], 'L0_xattn_W_q': _L0_xattn_in['W_q'], 'L0_xattn_b_q': _L0_xattn_in['b_q'], 'L0_xattn_W_o': _L0_xattn_in['W_o'], 'L0_xattn_b_o': _L0_xattn_in['b_o'], 'L0_ffn_w_gate': _L0_ffn_in['w_gate'], 'L0_ffn_b_gate': _L0_ffn_in['b_gate'], 'L0_ffn_W1': _L0_ffn_in['W1'], 'L0_ffn_b1': _L0_ffn_in['b1'], 'L0_ffn_W2': _L0_ffn_in['W2'], 'L0_ffn_b2': _L0_ffn_in['b2'], 'L1_attn_Wk': _L1_attn_in['Wk'], 'L1_attn_bk': _L1_attn_in['bk'], 'L1_attn_Wv': _L1_attn_in['Wv'], 'L1_attn_bv': _L1_attn_in['bv'], 'L1_attn_Wq': _L1_attn_in['Wq'], 'L1_attn_bq': _L1_attn_in['bq'], 'L1_attn_Wo': _L1_attn_in['Wo'], 'L1_attn_bo': _L1_attn_in['bo'], 'L1_xattn_Wq': _L1_xattn_in['Wq'], 'L1_xattn_bq': _L1_xattn_in['bq'], 'L1_xattn_Wk': _L1_xattn_in['Wk'], 'L1_xattn_bk': _L1_xattn_in['bk'], 'L1_xattn_Wo': _L1_xattn_in['Wo'], 'L1_xattn_bo': _L1_xattn_in['bo'], 'L1_ffn_Ws1': _L1_ffn_in['Ws1'], 'L1_ffn_Ws2': _L1_ffn_in['Ws2'], 'L1_ffn_W1': _L1_ffn_in['W1'], 'L1_ffn_W2': _L1_ffn_in['W2'], 'L1_ffn_Wr': _L1_ffn_in['Wr']}

def reference(x, ctx_1024, mask_BxSxS2_ik0, L0_attn_Wq, L0_attn_Wk, L0_attn_Wv, L0_xattn_W_kv, L0_xattn_b_kv, L0_xattn_W_q, L0_xattn_b_q, L0_xattn_W_o, L0_xattn_b_o, L0_ffn_w_gate, L0_ffn_b_gate, L0_ffn_W1, L0_ffn_b1, L0_ffn_W2, L0_ffn_b2, L1_attn_Wk, L1_attn_bk, L1_attn_Wv, L1_attn_bv, L1_attn_Wq, L1_attn_bq, L1_attn_Wo, L1_attn_bo, L1_xattn_Wq, L1_xattn_bq, L1_xattn_Wk, L1_xattn_bk, L1_xattn_Wo, L1_xattn_bo, L1_ffn_Ws1, L1_ffn_Ws2, L1_ffn_W1, L1_ffn_W2, L1_ffn_Wr):
    import jax
    import jax.numpy as jnp

    def _L0_attn_ref(x, Wq, Wk, Wv):
        import jax, jax.numpy as jnp
        import numpy as np
        B, N, D = (2, 256, 128)
        H, DK, DV = (8, 128, 128)
        n = x.shape[-2]
        Q = jnp.einsum('bnd,hed->bhne', x, Wq)
        K = jnp.einsum('bnd,hed->bhne', x, Wk)
        V = jnp.einsum('bnd,hvd->bhnv', x, Wv)
        scores = jnp.einsum('bhne,bhme->bhnm', Q, K)
        causal = jnp.tril(jnp.ones((n, n), dtype=bool))
        sim = jnp.where(causal, jax.nn.relu(scores), jnp.float32(0.0)) / jnp.float32(n)
        head_out = jnp.einsum('bhnm,bhmv->bnv', sim, V)
        return x + head_out

    def _L0_xattn_ref(x, y, mask, W_kv, b_kv, W_q, b_q, W_o, b_o):
        import jax, jax.numpy as jnp
        import numpy as np
        B, NKV, NQ, D, H = (4, 256, 128, 128, 16)
        HD = D // H
        b, nkv, _ = x.shape
        nq = y.shape[1]
        kv = x @ W_kv + b_kv
        q = y @ W_q + b_q
        kv = kv.reshape(b, nkv, H, 2 * HD).transpose(0, 2, 1, 3)
        q = q.reshape(b, nq, H, HD).transpose(0, 2, 1, 3)
        k, v = (kv[..., :HD], kv[..., HD:])
        scores = jnp.einsum('bhqd,bhkd->bhqk', q, k) / jnp.sqrt(jnp.float32(HD))
        scores = jnp.where(mask[:, None, :, :] == 0, jnp.float32(-1e+20), scores)
        attn = jax.nn.softmax(scores, axis=-1)
        vals = jnp.einsum('bhqk,bhkd->bhqd', attn, v)
        vals = vals.transpose(0, 2, 1, 3).reshape(b, nq, D)
        return vals @ W_o + b_o

    def _L0_ffn_ref(x, w_gate, b_gate, W1, b1, W2, b2):
        import jax, jax.numpy as jnp
        import numpy as np
        D_MODEL = 128
        MLP_DIM = 512
        N_EXPERTS = 8
        B, T = (4, 128)
        b, t, d = x.shape
        x_flat = x.reshape(b * t, d)
        logits = x_flat @ w_gate + b_gate
        probs = jax.nn.softmax(logits, axis=-1)
        route_p = jnp.max(probs, axis=-1)
        route_idx = jnp.argmax(probs, axis=-1)
        h = jnp.einsum('nd,edm->enm', x_flat, W1) + b1[:, None, :]
        h = jax.nn.relu(h)
        y = jnp.einsum('enm,emd->end', h, W2) + b2[:, None, :]
        n = b * t
        out = y[route_idx, jnp.arange(n)] * route_p[:, None]
        return out.reshape(b, t, d)

    def _L1_attn_ref(x, Wk, bk, Wv, bv, Wq, bq, Wo, bo):
        import jax, jax.numpy as jnp
        import numpy as np
        DECAY = 0.99
        LR = 0.01

        def _reference_tuple_inner(x, Wk, bk, Wv, bv, Wq, bq, Wo, bo):
            B, S, D = x.shape
            M = Wk.shape[0]
            k = jnp.einsum('bsd,md->bsm', x, Wk) + bk
            v = jnp.einsum('bsd,md->bsm', x, Wv) + bv
            q = jnp.einsum('bsd,md->bsm', x, Wq) + bq

            def step(state, kvq):
                k_t, v_t, q_t = kvq
                out_t = jnp.einsum('bij,bj->bi', state, q_t)
                state = DECAY * state + LR * jnp.einsum('bi,bj->bij', v_t, k_t)
                return (state, out_t)
            state0 = jnp.zeros((B, M, M), x.dtype)
            xs = (jnp.swapaxes(k, 0, 1), jnp.swapaxes(v, 0, 1), jnp.swapaxes(q, 0, 1))
            state, outs = jax.lax.scan(step, state0, xs)
            outs = jnp.swapaxes(outs, 0, 1)
            y = jnp.einsum('bsm,dm->bsd', outs, Wo) + bo
            return (y, state)
        return _reference_tuple_inner(x, Wk, bk, Wv, bv, Wq, bq, Wo, bo)[0]

    def _L1_xattn_ref(KV, Q, Wq, bq, Wk, bk, Wo, bo):
        import jax, jax.numpy as jnp
        import numpy as np
        B, KV_LEN, Q_LEN = (8, 256, 64)
        D, H = (128, 16)
        HD = D // H
        b, kv_len, _ = KV.shape
        q_len = Q.shape[1]
        q = (Q @ Wq + bq).reshape(b, q_len, H, HD)
        k = (KV @ Wk + bk).reshape(b, kv_len, H, HD)
        v = k
        scores = jnp.einsum('bqhd,bkhd->bhqk', q, k) / jnp.sqrt(jnp.float32(HD))
        attn = jax.nn.softmax(scores, axis=-2)
        ctx = jnp.einsum('bhqk,bkhd->bqhd', attn, v).reshape(b, q_len, D)
        return ctx @ Wo + bo

    def _L1_ffn_ref(x, Ws1, Ws2, W1, W2, Wr):
        import jax, jax.numpy as jnp
        import numpy as np
        D_MODEL = 128
        EXPERT_DIM = 64
        N_EXPERTS = 8
        TOP_K = 2

        def _sq_relu(h):
            return jnp.square(jax.nn.relu(h))
        shape = x.shape
        xf = x.reshape(-1, D_MODEL)
        out_shared = _sq_relu(xf @ Ws1) @ Ws2
        logits = xf @ Wr
        top_vals, top_idx = jax.lax.top_k(logits, TOP_K)
        rw = jax.nn.softmax(top_vals.astype(jnp.float32), axis=-1).astype(x.dtype)
        onehot = jax.nn.one_hot(top_idx, N_EXPERTS, dtype=x.dtype)
        prob = jnp.einsum('tk,tke->te', rw, onehot)
        prob = jnp.trunc(prob)
        h = _sq_relu(jnp.einsum('td,edf->tef', xf, W1))
        y = jnp.einsum('tef,efd->ted', h, W2)
        out_routed = jnp.einsum('ted,te->td', y, prob)
        return (out_shared + out_routed).reshape(shape)
    x = _layernorm(x + _L0_attn_ref(x, L0_attn_Wq, L0_attn_Wk, L0_attn_Wv), axis=-1)
    x = _layernorm(x + _L0_xattn_ref(ctx_1024, x, mask_BxSxS2_ik0, L0_xattn_W_kv, L0_xattn_b_kv, L0_xattn_W_q, L0_xattn_b_q, L0_xattn_W_o, L0_xattn_b_o), axis=-1)
    x = _layernorm(x + _L0_ffn_ref(x, L0_ffn_w_gate, L0_ffn_b_gate, L0_ffn_W1, L0_ffn_b1, L0_ffn_W2, L0_ffn_b2), axis=-1)
    x = _layernorm(x + _L1_attn_ref(x, L1_attn_Wk, L1_attn_bk, L1_attn_Wv, L1_attn_bv, L1_attn_Wq, L1_attn_bq, L1_attn_Wo, L1_attn_bo), axis=-1)
    x = _layernorm(x + _L1_xattn_ref(ctx_1024, x, L1_xattn_Wq, L1_xattn_bq, L1_xattn_Wk, L1_xattn_bk, L1_xattn_Wo, L1_xattn_bo), axis=-1)
    x = _layernorm(x + _L1_ffn_ref(x, L1_ffn_Ws1, L1_ffn_Ws2, L1_ffn_W1, L1_ffn_W2, L1_ffn_Wr), axis=-1)
    return x

_drawn_inputs = setup_inputs


def setup_inputs(seed=0):
    import zlib

    import numpy as np

    out = dict(_drawn_inputs(seed))
    spreads = {'L0_xattn_b_kv': (0.0, 0.382),
     'L0_xattn_b_q': (0.0, 2.0),
     'L0_xattn_b_o': (0.0, 0.1),
     'L0_ffn_b1': (0.0, 0.8),
     'L0_ffn_b2': (0.0, 0.34),
     'L1_attn_bk': (0.0, 0.58),
     'L1_attn_bv': (0.0, 0.541),
     'L1_attn_bq': (0.0, 0.8),
     'L1_attn_bo': (0.0, 0.1),
     'L1_xattn_bq': (0.0, 2.0),
     'L1_xattn_bk': (0.0, 0.1),
     'L1_xattn_bo': (0.0, 0.1)}
    factors = {'L0_attn_Wq': 5.021,
     'L0_attn_Wk': 5.022,
     'L0_attn_Wv': 4.358,
     'L0_xattn_W_q': 43.394,
     'L0_ffn_b_gate': 4.016,
     'L1_ffn_Ws1': 6.132,
     'L1_ffn_Ws2': 5.731}
    for name, (base, spread) in spreads.items():
        noise = np.random.default_rng([zlib.crc32(name.encode()), seed]).standard_normal(out[name].shape)
        drawn = base * np.exp(spread * noise) if base else spread * noise
        out[name] = jnp.asarray(drawn.astype(out[name].dtype))
    for name, factor in factors.items():
        out[name] = (out[name] * factor).astype(out[name].dtype)
    return out
```

```python
from contextlib import ExitStack

import numpy as np
import concourse.bass as bass
from concourse import mybir

F32 = mybir.dt.float32
BF16 = mybir.dt.bfloat16
I32 = mybir.dt.int32
U32 = mybir.dt.uint32
ALU = mybir.AluOpType
ACT = mybir.ActivationFunctionType
AX = mybir.AxisListType

B, S, D = 64, 64, 128
P = 128
TILES = B * S // P
PER = P // S
AH = 8
XH, HD = 16, 8
HALF = XH // 2
E0, M0 = 8, 512
CH = M0 // P
E1, M1 = 8, 64
EPS = 1e-5
ROWS = B * S
REGION = ROWS + P
UNROLL = 4
SLOTS = -(-(ROWS // P + E0 - 1) // UNROLL) * UNROLL
VW = HALF * HD + HALF


class Blob:

    def __init__(self, parts):
        self.at, self.width = {}, 0
        for name, n in parts:
            self.at[name] = (self.width, n)
            self.width += n

    def cols(self, ap, name):
        at, n = self.at[name]
        return ap[:, at:at + n]


FIRST = Blob([("wq_heads", AH * D), ("wk_heads", AH * D)])
WEIGHTS = Blob([
    ("ident", P), ("wv_t", AH * D), ("causal", S), ("head_of_row", HALF), ("expert_no", E0), ("region", E0), ("before", P),
    ("tile_rows", TILES), ("slot_no", SLOTS),
    ("ones_at", HALF // 2 * HALF),
    ("x0_wk", D), ("x0_wv", D), ("x0_wq", D), ("x0_wo", D), ("x0_bk", 1), ("x0_bq", 1), ("x0_bv", PER * D), ("x0_bo", D),
    ("gate_w", E0), ("gate_b", E0),
    ("a1_wk_t", D), ("a1_wq_t", D), ("a1_wv", D), ("a1_wo_t", D), ("a1_bk", 1), ("a1_bq", 1), ("a1_bv", 1), ("a1_bo", D),
    ("decay", P),
    ("x1_wq", D), ("x1_wk", D), ("x1_wo", D), ("x1_bq", 1), ("x1_bk", 1), ("x1_bk_row", D), ("x1_bo", D),
    ("shared_w1", M1), ("shared_w2", D), ("route_w", E1),
])


class Arrays:
    pass


class Kept:
    pass


class Tile:

    def __init__(self, q, m):
        self.q, self.m = q, m
        self.n = UNROLL * q + m


class Turn:

    def __init__(self, q, m, tiles=TILES):
        self.q, self.m, self.tiles = q, m, tiles
        self.n = UNROLL * q + m

    def tile(self, lag):
        up, m = divmod(self.m - lag, UNROLL)
        if isinstance(self.q, int) and not 0 <= self.n - lag < self.tiles:
            return None
        return Tile(self.q + up, m)


def wait(eng, sem, value):
    if isinstance(value, int) and value <= 0:
        return
    eng.wait_ge(sem, value)


class Chain:

    def __init__(self, eng, sem):
        self.eng, self.sem, self.count, self.turn = eng, sem, 0, None

    def mark(self, instruction):
        instruction.then_inc(self.sem, 1)
        self.count += 1
        return self.count

    def wait(self, mark):
        if self.turn is None:
            self.eng.wait_ge(self.sem, mark)
        else:
            i, per, less = self.turn
            self.eng.wait_ge(self.sem, i * per + (mark - less))

    def link(self, instruction):
        self.wait(self.mark(instruction))


def run_turns(eng, step, lags, chain=None, links=0, tiles=TILES, ahead=0):
    first, last = -(-(lags + ahead) // UNROLL), tiles // UNROLL
    for n in range(UNROLL * first):
        step(Turn(*divmod(n, UNROLL), tiles))
    before = chain.count if chain else 0
    with eng.Fori(first, last) as i:
        if chain:
            chain.turn = (i, UNROLL * links, UNROLL * links * first)
        for m in range(UNROLL):
            step(Turn(i, m, tiles))
    if chain:
        assert chain.count == before + UNROLL * links, (chain.count - before) / UNROLL
        chain.turn, chain.count = None, before + UNROLL * links * (last - first)
    for n in range(UNROLL * last, tiles + lags):
        step(Turn(*divmod(n, UNROLL), tiles))


def split_heads(ap):
    return ap.rearrange("p (h n) -> p h n", h=HALF)


def spread(ap, axis, n):
    names = ["p", "a", "b"][:len(ap.shape)]
    to = names[:axis] + ["o"] + names[axis:]
    merged = names[:axis] + ["(o " + names[axis] + ")"] + names[axis + 1:] if axis < len(names) else names[:-1] + ["(" + names[-1] + " o)"]
    shape = list(ap.shape)
    return ap.rearrange(" ".join(merged) + " -> " + " ".join(to), o=1).broadcast_to(shape[:axis] + [n] + shape[axis:])


class Norm:

    def __init__(self, new, sems, name, lanes):
        self.sum = [new(f"{name}_sum{k}", [P, D]) for k in range(lanes)]
        self.stats = new(f"{name}_stats", [P, lanes, 6])
        self.moments = new(f"{name}_moments", [P, lanes, 2])
        self.var = new(f"{name}_var", [P, lanes])
        self.log = new(f"{name}_log", [P, lanes])
        self.guess = new(f"{name}_guess", [P, lanes])
        self.half = new(f"{name}_half", [P, lanes])
        self.rstd = new(f"{name}_rstd", [P, lanes])
        self.idle = new(f"{name}_idle", [P, 2])
        self.var_ready, self.guess_ready, self.log_ready = (sems(f"{name}_{x}") for x in ("var_ready", "guess_ready", "log_ready"))


def norm_scalar(act, norm, count, a, b):
    act.wait_ge(norm.var_ready, count)
    act.activation(norm.log[:, a:b], norm.var[:, a:b], ACT.Ln).then_inc(norm.log_ready, 1)
    act.wait_ge(norm.log_ready, count)
    act.activation(norm.guess[:, a:b], norm.log[:, a:b], ACT.Exp, scale=-0.5).then_inc(norm.guess_ready, 1)


def norm_vector(dve, chain, norm, count, lanes):
    ks = [lane[0] for lane in lanes]
    a, b = min(ks), max(ks) + 1
    for k in ks:
        stats = dve.bn_stats(norm.stats[:, k, :], norm.sum[k][:, :])
    chain.link(stats)
    dve.tensor_copy(norm.idle[:, 0:1], norm.idle[:, 1:2])
    for k in ks:
        last = chain.mark(dve.bn_aggr(norm.moments[:, k, :], norm.stats[:, k, :]))
    chain.wait(last)
    dve.tensor_scalar(norm.var[:, a:b], norm.moments[:, a:b, 1], EPS, None, ALU.add).then_inc(norm.var_ready, 1)
    dve.wait_ge(norm.guess_ready, count)
    guess = norm.guess[:, a:b]
    chain.link(dve.scalar_tensor_tensor(norm.half[:, a:b], guess, -0.5, guess, ALU.mult, ALU.mult))
    chain.link(dve.tensor_tensor(norm.half[:, a:b], norm.half[:, a:b], norm.var[:, a:b], ALU.mult))
    chain.link(dve.scalar_tensor_tensor(norm.rstd[:, a:b], norm.half[:, a:b], 1.5, guess, ALU.add, ALU.mult))
    for k, out, sem, before in lanes:
        before()
        dve.tensor_scalar(out, norm.sum[k][:, :], norm.moments[:, k, 0:1], norm.rstd[:, k:k + 1],
                          ALU.subtract, ALU.mult).then_inc(sem, 1)


def pick(ap, t):
    at = slice(t.n, t.n + 1) if isinstance(t.n, int) else bass.ds(t.n, 1)
    return ap[(slice(None), at) + (slice(None),) * (len(ap.shape) - 2)]


def plane(ap, n):
    return ap[n, :, :] if isinstance(n, int) else ap[bass.ds(n, 1), :, :].rearrange("o p n -> p (o n)")


LINKS_A = 12


def turned_count(j, lags=(2, 4, 5)):
    if isinstance(j.n, int):
        return sum(min(max(j.n - lag + 1, 0), j.tiles) for lag in lags)
    return len(lags) * UNROLL * j.q + (len(lags) * (j.m + 1) - sum(lags))


def layer0_attention(nc, io, keep):
    with ExitStack() as ctx:
        new = lambda name, shape, dt=F32: ctx.enter_context(nc.sbuf_tensor(name, shape, dt))
        sems = lambda name: ctx.enter_context(nc.semaphore(name))
        w = lambda name: WEIGHTS.cols(keep.weights, name)
        ps = ctx.enter_context(nc.psum_tensor("ps", [P, 8, 512], F32))

        heads_w = new("heads_w", [P, FIRST.width])
        wqk = new("wqk", [P, AH * D])
        mask = new("mask", [P, TILES, S], I32)
        mask_add = new("mask_add", [P, TILES, S])
        alive = new("alive", [P, TILES])
        bq_scaled = new("bq_scaled", [P, 1])
        before_b = new("before_b", [P, P], BF16)
        ones_b = new("ones_b", [P, P], BF16)
        base = keep.base

        x_nat = [new(f"x_nat{m}", [P, D]) for m in range(UNROLL)]
        x_t = [new(f"x_t{m}", [P, P]) for m in range(UNROLL)]
        ctx_t = [new(f"ctx_t{m}", [P, PER, 2, S]) for m in range(UNROLL)]
        g = new("g", [P, AH, P])
        v = new("v", [P, AH * D])
        sim = new("sim", [P, AH, P])
        x1 = [new(f"x1_{m}", [P, D]) for m in range(2)]
        x1_plus = [new(f"x1_plus{m}", [P, D]) for m in range(UNROLL)]
        q_t = new("q_t", [P, P])
        k_t = new("k_t", [P, P])
        k_heads = new("k_heads", [P, HALF, P])
        e = [new(f"e{m}", [P, XH, S]) for m in range(2)]
        row_max = [new(f"row_max{m}", [P, XH]) for m in range(2)]
        e_t = new("e_t", [P, XH // 2, P])
        v_heads = new("v_heads", [P, PER * 2, HALF // 2 * (VW + 2 * HD)])
        rden = new("rden", [P, 2, HALF])
        mixed = new("mixed", [P, D])
        x2 = [new(f"x2_{m}", [P, D]) for m in range(UNROLL)]
        turned_t = new("turned_t", [P, 3 * P])
        lg = [new(f"lg{m}", [P, E0]) for m in range(UNROLL)]
        top = new("top", [P, 8])
        top_at = new("top_at", [P, 8], U32)
        top_f = new("top_f", [P, 1])
        chosen = new("chosen", [P, E0], BF16)
        rows8 = new("rows8", [P, E0])
        rows8c = new("rows8c", [P, E0])
        row_f = new("row_f", [P, 1])
        row_i = [new(f"row_i{m}", [P, 1], I32) for m in range(UNROLL)]
        norm = Norm(new, sems, "n0", 2)

        weights_loaded, first_loaded = sems("weights_loaded"), sems("first_loaded")
        mask_loaded = sems("mask_loaded")
        fused, wqk_ready, const_ready = sems("fused"), sems("wqk_ready"), sems("const_ready")
        x_loaded = [sems(f"x_loaded{m}") for m in range(UNROLL)]
        x2_stored = [sems(f"x2_stored{m}") for m in range(UNROLL)]
        scattered = [sems(f"scattered{m}") for m in range(UNROLL)]
        (g_done, g_ready, v_done, v_ready, st_done, sim_ready, av_done, attn_added, x1_ready, turned_done, turned_ready,
         q_done, qt_ready, k_done, kt_ready, kexp_ready, v2_done, vexp_ready, s_done, s_read, max_ready, sub_ready,
         e_ready, et_done, et_ready, avx_done, mixed_ready, side_done, x1p_ready,
         xattn_added, x2_ready, lg_read, lg_kept, chosen_ready, rank_done, base_added, row_ready,
         dve_chain) = (sems(n) for n in (
             "g_done", "g_ready", "v_done", "v_ready", "st_done", "sim_ready", "av_done", "attn_added", "x1_ready",
             "turned_done", "turned_ready", "q_done", "qt_ready", "k_done", "kt_ready", "kexp_ready", "v2_done",
             "vexp_ready", "s_done", "s_read", "max_ready", "sub_ready", "e_ready", "et_done", "et_ready",
             "avx_done", "mixed_ready", "side_done", "x1p_ready", "xattn_added",
             "x2_ready", "lg_read", "lg_kept", "chosen_ready", "rank_done", "base_added",
             "row_ready", "dve_chain"))

        g_ps = ps[:, 0:2, :].rearrange("p a n -> p (a n)")
        st_ps = ps[:, 0, :].rearrange("p (h n) -> p h n", h=AH)
        z_ps = ps[:, 0, 0:D]
        v2_ps = ps[:, 1, 0:PER * D]
        v_ps = ps[:, 2:4, :].rearrange("p a n -> p (a n)")
        s_ps = ps[:, 4:6, :]
        mix_ps = ps[:, 4, 0:2 * VW].rearrange("p (g n) -> p g n", g=2)
        turned_ps = ps[:, 6, 0:3 * P]
        q_ps = k_ps = ps[:, 6, 0:P]
        wo_ps = ps[:, 7, 0:D]
        lg_ps = ps[:, 7, P:P + E0]
        rank_ps, total_ps = (ps[:, 7, k * E0:(k + 1) * E0] for k in range(2))

        block = ctx.enter_context(nc.Block())

        @block.sync
        def _(sp):
            sp.dma_start(heads_w[:, :], io.first).then_inc(first_loaded, 16)
            sp.dma_start(keep.weights[:, :], io.weights).then_inc(weights_loaded, 16)

            def step(j):
                if t := j.tile(0):
                    wait(sp, attn_added, t.n - UNROLL + 1)
                    wait(sp, v2_done, t.n - UNROLL + 1)
                    sp.dma_start(x_t[t.m][:, :], plane(io.x_t, t.n)).then_inc(x_loaded[t.m], 16)
                    sp.dma_start(x_nat[t.m][:, :], plane(io.x, t.n)).then_inc(x_loaded[t.m], 16)
                    sp.dma_start(ctx_t[t.m][:, :, :, :].rearrange("p b c n -> p (b c n)"),
                                 plane(io.ctx_t, t.n)).then_inc(x_loaded[t.m], 16)
                if isinstance(j.n, int) and j.n == 1:
                    sp.dma_start(mask[:, :, :], io.mask).then_inc(mask_loaded, 16)
                if t := j.tile(5):
                    wait(sp, x2_ready, t.n + 1)
                    sp.dma_start(plane(io.x2, t.n), x2[t.m][:, :]).then_inc(x2_stored[t.m], 16)

            run_turns(sp, step, 6)
            for m in range(UNROLL):
                sp.wait_ge(x2_stored[m], 16 * TILES // UNROLL)

        @block.tensor
        def _(pe):
            pe.wait_ge(first_loaded, 16)
            for h in range(AH):
                part = FIRST.cols(heads_w, "wq_heads"), FIRST.cols(heads_w, "wk_heads")
                pe.matmul(g_ps[:, h * D:(h + 1) * D], part[0][:, h * D:(h + 1) * D], part[1][:, h * D:(h + 1) * D],
                          start=True, stop=True).then_inc(fused, 1)
            pe.wait_ge(wqk_ready, 2)
            pe.wait_ge(weights_loaded, 16)
            pe.wait_ge(const_ready, 1)
            ident = w("ident")
            turned = ((2, x1_ready, x1), (4, mixed_ready, [mixed]), (5, x2_ready, x2))

            def step(j):
                if t := j.tile(1):
                    pe.wait_ge(x_loaded[t.m], 48 * (t.q + 1))
                    wait(pe, attn_added, t.n)
                    wait(pe, vexp_ready, 2 * (t.n - 2))
                    for h in range(AH):
                        mm = pe.matmul(g_ps[:, h * P:(h + 1) * P], wqk[:, h * D:(h + 1) * D], x_t[t.m][:, :],
                                       start=True, stop=True)
                        if h % 4 == 3:
                            mm.then_inc(g_done, 1)
                wait(pe, kt_ready, j.n - 1 if not isinstance(j.n, int) else min(j.n - 1, TILES))
                for k, (lag, ready, src) in enumerate(turned):
                    if t := j.tile(lag):
                        pe.wait_ge(ready, t.n + 1)
                        pe.transpose(turned_ps[:, k * P:(k + 1) * P], src[t.m % len(src)][:, :],
                                     ident).then_inc(turned_done, 1)
                if t := j.tile(1):
                    for c in range(2):
                        pe.matmul(v_ps[:, c * 512:(c + 1) * 512], x_t[t.m][:, :], w("wv_t")[:, c * 512:(c + 1) * 512],
                                  start=True, stop=True).then_inc(v_done, 1)
                if t := j.tile(2):
                    pe.wait_ge(turned_ready, t.n + 1)
                    pe.matmul(q_ps, w("x0_wq"), turned_t[:, 0:P], start=True, stop=True).then_inc(q_done, 1)
                if t := j.tile(1):
                    pe.wait_ge(g_ready, 2 * t.n + 2)
                    for b in range(PER):
                        mm = pe.matmul(st_ps[b * S:(b + 1) * S, :, :], x_t[t.m][:, b * S:(b + 1) * S],
                                       g[:, :, b * S:(b + 1) * S], start=True, stop=True)
                    mm.then_inc(st_done, 1)
                if t := j.tile(4):
                    pe.wait_ge(turned_ready, t.n + 3)
                    wait(pe, base_added, t.n - 1)
                    wait(pe, xattn_added, t.n)
                    mm = pe.matmul(wo_ps, turned_t[:, P:2 * P], w("x0_wo"), start=True, stop=True)
                if t := j.tile(5):
                    pe.wait_ge(turned_ready, t.n + 4)
                    wait(pe, base_added, t.n)
                    wait(pe, xattn_added, t.n + 1)
                    mm = pe.matmul(lg_ps, turned_t[:, 2 * P:3 * P], w("gate_w"), start=True, stop=True)
                if j.tile(4) or j.tile(5):
                    mm.then_inc(side_done, 1)
                if t := j.tile(2):
                    pe.wait_ge(qt_ready, t.n + 1)
                    pe.wait_ge(kexp_ready, t.n + 1)
                    wait(pe, s_read, t.n)
                    wait(pe, mixed_ready, t.n - 1)
                if t := j.tile(3):
                    for b in range(PER):
                        mm = pe.matmul(v2_ps[:, b * D:(b + 1) * D], ctx_t[t.m][:, b, :, :].rearrange("p c n -> p (c n)"),
                                       w("x0_wv"), start=True, stop=True)
                    mm.then_inc(v2_done, 1)
                if t := j.tile(2):
                    for r in range(2):
                        for b in range(PER):
                            mm = pe.matmul(s_ps[b * S:(b + 1) * S, r, :], q_t[r * S:(r + 1) * S, b * S:(b + 1) * S],
                                           k_heads[r * S:(r + 1) * S, :, b * S:(b + 1) * S], start=True, stop=True)
                    mm.then_inc(s_done, 1)
                if t := j.tile(1):
                    pe.wait_ge(sim_ready, 2 * t.n + 2)
                    pe.wait_ge(v_ready, 2 * t.n + 2)
                    for h in range(AH):
                        mm = pe.matmul(z_ps, sim[:, h, :], v[:, h * D:(h + 1) * D], start=(h == 0), stop=(h == AH - 1))
                    mm.then_inc(av_done, 1)
                if t := j.tile(3):
                    pe.wait_ge(e_ready, t.n + 1)
                    wait(pe, v_ready, 2 * (t.n + 3) if not isinstance(t.n, int) else 2 * min(t.n + 3, TILES))
                    e_flat = e[t.m % 2][:, :, :].rearrange("p h n -> p (h n)")
                    for c in range(XH // 2):
                        mm = pe.transpose(v_ps[:, c * P:(c + 1) * P], e_flat[:, c * P:(c + 1) * P], ident)
                        if c % 4 == 3:
                            mm.then_inc(et_done, 1)
                if t := j.tile(1):
                    wait(pe, kt_ready, t.n)
                    pe.matmul(k_ps, w("x0_wk"), ctx_t[t.m][:, :, 0, :], start=True, stop=True).then_inc(k_done, 1)
                if t := j.tile(3):
                    pe.wait_ge(vexp_ready, 2 * t.n + 2)
                    wait(pe, s_read, t.n + 2 if not isinstance(t.n, int) else min(t.n + 2, TILES))
                    for c in range(XH // 2):
                        if c % 4 == 0:
                            pe.wait_ge(et_ready, 2 * t.n + c // 4 + 1)
                        for b in range(PER):
                            mm = pe.matmul(mix_ps[b * S:(b + 1) * S, c // 4, :], e_t[:, c, b * S:(b + 1) * S],
                                           v_heads[:, 2 * b + c // 4, c % 4 * VW:(c % 4 + 1) * VW],
                                           start=(c % 4 == 0), stop=(c % 4 == 3))
                    mm.then_inc(avx_done, 1)
                if t := j.tile(5):
                    pe.wait_ge(chosen_ready, t.n + 1)
                    wait(pe, lg_read, t.n + 1)
                    wait(pe, xattn_added, t.n + 2 if not isinstance(t.n, int) else min(t.n + 2, TILES))
                    pe.matmul(rank_ps, before_b[:, :], chosen[:, :], start=True, stop=True)
                    pe.matmul(total_ps, ones_b[:, :], chosen[:, :], start=True, stop=True).then_inc(rank_done, 1)

            run_turns(pe, step, 6)

        @block.scalar
        def _(act):
            act.preload_act_table_set("natural_log_exp_and_others")
            act.dma_start(keep.w1[:, :, :], io.w1).then_inc(keep.ffn_loaded, 16)
            act.dma_start(keep.w2[:, :, :, :], io.w2).then_inc(keep.ffn_loaded, 16)
            act.dma_start(keep.b1[:, :, :], io.b1).then_inc(keep.ffn_loaded, 16)
            act.dma_start(keep.b2[:, :, :], io.b2).then_inc(keep.ffn_loaded, 16)
            for c in range(2):
                act.wait_ge(fused, 4 * c + 4)
                act.activation(wqk[:, c * 512:(c + 1) * 512], g_ps[:, c * 512:(c + 1) * 512],
                               ACT.Copy).then_inc(wqk_ready, 1)
            act.wait_ge(const_ready, 1)

            def step(j):
                if t := j.tile(1):
                    for c in range(2):
                        act.wait_ge(g_done, 2 * t.n + c + 1)
                        act.activation(g[:, 4 * c:4 * c + 4, :].rearrange("p h n -> p (h n)"),
                                       g_ps[:, c * 512:(c + 1) * 512], ACT.Copy).then_inc(g_ready, 1)
                here = [k for k, lag in enumerate((2, 4, 5)) if j.tile(lag)]
                if here:
                    act.wait_ge(turned_done, turned_count(j))
                    r = slice(here[0] * P, (here[-1] + 1) * P)
                    act.activation(turned_t[:, r], turned_ps[:, r], ACT.Copy).then_inc(turned_ready, 1)
                if t := j.tile(3):
                    act.wait_ge(sub_ready, t.n + 1)
                    act.activation(e[t.m % 2][:, :, :], e[t.m % 2][:, :, :], ACT.Exp).then_inc(e_ready, 1)
                if t := j.tile(1):
                    for c in range(2):
                        act.wait_ge(v_done, 2 * t.n + c + 1)
                        act.activation(v[:, c * 512:(c + 1) * 512], v_ps[:, c * 512:(c + 1) * 512],
                                       ACT.Copy).then_inc(v_ready, 1)
                if t := j.tile(2):
                    act.wait_ge(q_done, t.n + 1)
                    act.activation(q_t[:, :], q_ps, ACT.Identity, bias=bq_scaled[:, 0:1],
                                   scale=HD ** -0.5).then_inc(qt_ready, 1)
                if t := j.tile(3):
                    act.wait_ge(et_done, 2 * t.n + 1)
                    act.activation(e_t[:, 0:4, :].rearrange("p h n -> p (h n)"), v_ps[:, 0:512],
                                   ACT.Copy).then_inc(et_ready, 1)
                if j.tile(1) or j.tile(4):
                    norm_scalar(act, norm, j.n, 0 if j.tile(1) else 1, 2 if j.tile(4) else 1)
                if t := j.tile(3):
                    act.wait_ge(et_done, 2 * t.n + 2)
                    act.activation(e_t[:, 4:8, :].rearrange("p h n -> p (h n)"), v_ps[:, 512:1024],
                                   ACT.Copy).then_inc(et_ready, 1)
                if t := j.tile(1):
                    act.wait_ge(k_done, t.n + 1)
                    wait(act, kexp_ready, t.n)
                    act.activation(k_t[:, :], k_ps, ACT.Identity, bias=w("x0_bk")).then_inc(kt_ready, 1)

            run_turns(act, step, 6)

        @block.gpsimd
        def _(pool):
            pool.wait_ge(weights_loaded, 16)

            def step(j):
                if t := j.tile(2):
                    pool.wait_ge(kt_ready, t.n + 1)
                    wait(pool, s_done, t.n)
                    pool.tensor_tensor(k_heads[:, :, :], spread(k_t[:, :], 1, HALF),
                                       spread(w("head_of_row"), 2, P), ALU.mult).then_inc(kexp_ready, 1)
                if t := j.tile(6):
                    pool.wait_ge(row_ready, t.n + 1)
                if t := j.tile(2):
                    pool.wait_ge(x1_ready, t.n + 1)
                    wait(pool, xattn_added, t.n - UNROLL + 1)
                    pool.tensor_tensor(x1_plus[t.m][:, :], x1[t.m % 2][:, :], w("x0_bo"), ALU.add).then_inc(x1p_ready, 1)
                if t := j.tile(6):
                    pool.indirect_dma_start(io.sorted, bass.IndirectOffsetOnAxis(ap=row_i[t.m][:, 0:1], axis=0),
                                            x2[t.m][:, :], None).then_inc(scattered[t.m], 16)
                if t := j.tile(5):
                    pool.wait_ge(lg_read, t.n + 1)
                    pool.tensor_copy(pick(keep.logits, t).rearrange("p o n -> p (o n)"), lg[t.m][:, :]).then_inc(lg_kept, 1)
                if t := j.tile(2):
                    pool.wait_ge(max_ready, t.n + 1)
                    pool.tensor_tensor(e[t.m % 2][:, :, :], e[t.m % 2][:, :, :], spread(row_max[t.m % 2][:, :], 2, S),
                                       ALU.subtract).then_inc(sub_ready, 1)

            run_turns(pool, step, 6)
            for m in range(UNROLL):
                pool.wait_ge(scattered[m], 16 * TILES // UNROLL)

        @block.vector
        def _(dve):
            chain = Chain(dve, dve_chain)
            dve.memset(sim[:, :, :], 0.0)
            dve.memset(norm.idle[:, :], 0.0)
            dve.memset(v_heads[:, :, :], 0.0)
            dve.memset(ones_b[:, :], 1.0)
            dve.wait_ge(weights_loaded, 16)
            dve.tensor_copy(before_b[:, :], w("before"))
            dve.tensor_copy(base[:, :], w("region"))
            zeroed = chain.mark(dve.tensor_scalar(bq_scaled[:, :], w("x0_bq"), HD ** -0.5, None, ALU.mult))
            chain.wait(zeroed)
            for half in range(PER * 2):
                pairs = v_heads[:, half, 0:HALF // 2 * VW].rearrange("p (c n) -> p c n", n=VW)
                last = dve.tensor_copy(pairs[:, :, HALF * HD:VW], w("ones_at").rearrange("p (c n) -> p c n", n=HALF))
            last.then_inc(const_ready, 1)
            dve.wait_ge(mask_loaded, 16)
            chain.link(dve.tensor_scalar(mask_add[:, :, :], mask[:, :, :], 0, -1e20, ALU.is_equal, ALU.mult))
            chain.link(dve.tensor_reduce(alive[:, :], mask_add[:, :, :], axis=AX.X, op=ALU.max))
            chain.link(dve.tensor_scalar(alive[:, :], alive[:, :], 0.0, None, ALU.is_equal))
            chain.link(dve.tensor_tensor(mask_add[:, :, :], mask_add[:, :, :], spread(alive[:, :], 2, S), ALU.mult))

            def value_half(r):
                rows = slice(r * S, (r + 1) * S)
                pairs = "p (g c h n) -> p g c h n"
                src = v2_ps[rows, :].rearrange(pairs, g=2 * PER, c=HALF // 2, h=2)[:, :, :, r, :]
                bias = w("x0_bv")[rows, :].rearrange(pairs, g=2 * PER, c=HALF // 2, h=2)[:, :, :, r, :]
                own = v_heads[rows, :, :].rearrange("p g (c n) -> p g c n", c=HALF // 2)[:, :, :, r * HD:(r + 1) * HD]
                dve.tensor_tensor(own, src, bias, ALU.add).then_inc(vexp_ready, 1)

            def step(j):
                if t := j.tile(6):
                    dve.wait_ge(rank_done, t.n + 1)
                    rows_sum = chain.mark(dve.tensor_tensor(rows8[:, :], rank_ps, base[:, :], ALU.add))
                    dve.tensor_tensor(base[:, :], base[:, :], total_ps, ALU.add).then_inc(base_added, 1)
                    chain.wait(rows_sum)
                    row = chain.mark(dve.tensor_tensor_reduce(out=rows8c[:, :], in0=rows8[:, :], in1=chosen[:, :],
                                                              scale=1.0, scalar=0.0, op0=ALU.mult, op1=ALU.add,
                                                              accum_out=row_f[:, 0:1]))

                def masked(t, b):
                    r = slice(b * S, (b + 1) * S)
                    dve.scalar_tensor_tensor(sim[r, :, r], st_ps[r, :, :], 0.0, spread(w("causal")[r, :], 1, AH),
                                             ALU.max, ALU.mult).then_inc(sim_ready, 1)

                if t := j.tile(1):
                    dve.wait_ge(st_done, t.n + 1)
                    masked(t, 0)
                if t := j.tile(6):
                    chain.wait(row)
                    wait(dve, scattered[t.m], 16 * t.q)
                    dve.tensor_copy(row_i[t.m][:, :], row_f[:, :]).then_inc(row_ready, 1)
                    dve.tensor_copy(pick(keep.rows[:, :], t), row_f[:, :])
                if t := j.tile(5):
                    dve.wait_ge(side_done, t.n + 2)
                    wait(dve, lg_kept, t.n - 1)
                    dve.tensor_tensor(lg[t.m][:, :], lg_ps, w("gate_b"), ALU.add).then_inc(lg_read, 1)
                    dve.wait_ge(lg_read, t.n + 1)
                if t := j.tile(1):
                    masked(t, 1)
                if t := j.tile(5):
                    topped = chain.mark(dve.max(out=top[:, :], in_=lg[t.m][:, :]))
                if t := j.tile(3):
                    dve.wait_ge(v2_done, t.n + 1)
                    wait(dve, avx_done, t.n)
                    value_half(0)
                    value_half(1)
                if j.tile(5):
                    chain.wait(topped)
                if t := j.tile(2):
                    dve.wait_ge(s_done, t.n + 1)
                    wait(dve, et_done, 2 * (t.n - 1))
                    dve.scalar_tensor_tensor(e[t.m % 2][:, :, :], s_ps[:, :, :].rearrange("p r (h n) -> p (r h) n", h=HALF),
                                             pick(alive, t), pick(mask_add, t).broadcast_to([P, XH, S]),
                                             ALU.mult, ALU.add).then_inc(s_read, 1)
                if t := j.tile(5):
                    found = chain.mark(dve.max_index(out=top_at[:, :], in_max=top[:, :], in_values=lg[t.m][:, :]))
                if t := j.tile(2):
                    dve.wait_ge(s_read, t.n + 1)
                    wait(dve, sub_ready, t.n - 1)
                    dve.tensor_reduce(row_max[t.m % 2][:, :], e[t.m % 2][:, :, :], axis=AX.X, op=ALU.max).then_inc(max_ready, 1)
                if t := j.tile(5):
                    chain.wait(found)
                    chain.link(dve.tensor_copy(top_f[:, :], top_at[:, 0:1]))
                    wait(dve, rank_done, t.n)
                    dve.tensor_scalar(chosen[:, :], w("expert_no"), top_f[:, 0:1], None,
                                      ALU.is_equal).then_inc(chosen_ready, 1)
                lanes = []
                if t := j.tile(4):
                    dve.wait_ge(side_done, t.n + 1)
                    dve.wait_ge(x1p_ready, t.n + 1)
                    dve.tensor_tensor(norm.sum[1][:, :], wo_ps, x1_plus[t.m][:, :], ALU.add).then_inc(xattn_added, 1)
                    def free2(t=t):
                        wait(dve, x2_stored[t.m], 16 * t.q)
                        wait(dve, scattered[t.m], 16 * t.q)
                    lanes.append((1, x2[t.m][:, :], x2_ready, free2))
                if t := j.tile(1):
                    dve.wait_ge(av_done, t.n + 1)
                    dve.scalar_tensor_tensor(norm.sum[0][:, :], x_nat[t.m][:, :], 2.0, z_ps, ALU.mult,
                                             ALU.add).then_inc(attn_added, 1)
                    def free1(t=t):
                        wait(dve, x1p_ready, t.n - 1)
                    lanes.append((0, x1[t.m % 2][:, :], x1_ready, free1))
                if lanes:
                    lanes.sort(key=lambda lane: lane[0])
                    if t := j.tile(4):
                        dve.wait_ge(xattn_added, t.n + 1)
                    if t := j.tile(1):
                        dve.wait_ge(attn_added, t.n + 1)
                    norm_vector(dve, chain, norm, j.n, lanes)
                if t := j.tile(3):
                    dve.wait_ge(avx_done, t.n + 1)
                    chain.link(dve.reciprocal(rden[:, :, :], mix_ps[:, :, HALF * HD:VW]))
                    dve.tensor_tensor(mixed[:, :].rearrange("p (g h n) -> p g h n", g=2, h=HALF),
                                      mix_ps[:, :, 0:HALF * HD].rearrange("p g (h n) -> p g h n", h=HALF),
                                      spread(rden[:, :, :], 3, HD), ALU.mult).then_inc(mixed_ready, 1)

            run_turns(dve, step, 6, chain, LINKS_A)


LINKS_B = 0


def layer0_experts(nc, io, keep):
    with ExitStack() as ctx:
        new = lambda name, shape, dt=F32: ctx.enter_context(nc.sbuf_tensor(name, shape, dt))
        sems = lambda name: ctx.enter_context(nc.semaphore(name))
        w = lambda name: WEIGHTS.cols(keep.weights, name)
        ps = ctx.enter_context(nc.psum_tensor("ps_b", [P, 8, 512], F32))
        idle = SLOTS - ROWS // P
        dummy = E0 * REGION

        count = new("count", [P, E0])
        fills = new("fills", [P, E0, TILES])
        slots = new("slots", [P, E0])
        less = new("less", [P, E0])
        rows_f = new("rows_f", [P, TILES])
        behind = new("behind", [P, TILES, E0])
        skipped = new("skipped", [P, TILES])
        ends = [new(f"ends{k}", [1, E0]) for k in range(1, 4)]
        first_row = new("first_row", [1, E0])
        past = new("past", [1, SLOTS, E0])
        expert_f = new("expert_f", [1, SLOTS])
        unused = new("unused", [1, SLOTS])
        row_f = new("row_f_b", [1, SLOTS])
        expert_i = new("expert_i", [1, SLOTS], I32)
        row_i = new("row_i_b", [1, SLOTS], I32)
        pad_i = new("pad_i", [1, E0], I32)
        zeros = new("zeros", [P, D])
        best = new("best", [P, TILES])
        shifted = new("shifted", [P, TILES, E0])
        total = new("total", [P, TILES])

        xs = [new(f"xs{m}", [P, D]) for m in range(UNROLL)]
        xs_t = new("xs_t", [P, P])
        h = [new(f"h{m}", [P, M0]) for m in range(2)]
        h_t = new("h_t", [P, CH, P])
        y = [new(f"y{m}", [P, D]) for m in range(UNROLL)]

        loaded = [sems(f"xs_loaded{m}") for m in range(UNROLL)]
        stored = [sems(f"y_stored{m}") for m in range(UNROLL)]
        (tables_ready, pads_zeroed, xt_done, xt_ready, h_done, h_ready, ht_done, ht_ready, y_done, y_ready,
         best_ready, exp_ready, chain_b) = (sems(n) for n in (
             "tables_ready", "pads_zeroed", "xt_done", "xt_ready", "h_done", "h_ready", "ht_done",
             "ht_ready", "y_done", "y_ready", "best_ready", "exp_ready", "chain_b"))

        block = ctx.enter_context(nc.Block())

        def number(eng, table, t, most):
            at = slice(t.n, t.n + 1) if isinstance(t.n, int) else bass.ds(t.n, 1)
            return eng.value_load(table[0:1, at], min_val=0, max_val=most)

        @block.sync
        def _(sp):
            sp.wait_ge(tables_ready, 1)
            for k in range(E0):
                row = sp.value_load(pad_i[0:1, k:k + 1], min_val=0, max_val=dummy + (idle - 1) * P)
                sp.dma_start(io.sorted[bass.ds(row, P), :], zeros[:, :]).then_inc(pads_zeroed, 16)
            for k in range(idle):
                sp.dma_start(io.sorted[dummy + k * P:dummy + (k + 1) * P, :], zeros[:, :]).then_inc(pads_zeroed, 16)
            sp.wait_ge(pads_zeroed, 16 * (E0 + idle))

            def step(j):
                if t := j.tile(0):
                    wait(sp, xt_done, t.n - UNROLL + 1)
                    row = number(sp, row_i, t, dummy + (idle - 1) * P)
                    sp.dma_start(xs[t.m][:, :], io.sorted[bass.ds(row, P), :]).then_inc(loaded[t.m], 16)
                if t := j.tile(4):
                    sp.wait_ge(y_ready, t.n + 1)
                    sp.dma_start(plane(io.y.rearrange("(t p) d -> t p d", p=P), t.n), y[t.m][:, :]).then_inc(stored[t.m], 16)

            run_turns(sp, step, 4, tiles=SLOTS, ahead=2)
            for m in range(UNROLL):
                sp.wait_ge(stored[m], 16 * SLOTS // UNROLL)
            sp.wait_ge(keep.ffn_loaded, 64)

        @block.tensor
        def _(pe):
            pe.wait_ge(keep.ffn_loaded, 64)
            pe.wait_ge(tables_ready, 1)

            def step(j):
                if t := j.tile(1):
                    pe.wait_ge(loaded[t.m], 16 * (t.q + 1))
                    wait(pe, xt_ready, t.n - 1)
                    pe.transpose(ps[:, t.m % 2, 0:P], xs[t.m][:, :], w("ident")).then_inc(xt_done, 1)
                if t := j.tile(4):
                    expert = number(pe, expert_i, t, E0 - 1)
                    pe.wait_ge(ht_ready, t.n + 1)
                    wait(pe, y_ready, t.n - 1)
                    for c in range(CH):
                        mm = pe.matmul(ps[:, 6 + t.m % 2, 0:D], h_t[:, c, :],
                                       keep.w2[:, bass.ds(expert, 1), c, :].rearrange("p o n -> p (o n)"),
                                       start=(c == 0), stop=(c == CH - 1))
                    mm.then_inc(y_done, 1)
                if t := j.tile(2):
                    expert = number(pe, expert_i, t, E0 - 1)
                    pe.wait_ge(xt_ready, t.n + 1)
                    wait(pe, h_ready, t.n - 1)
                    pe.matmul(ps[:, 2 + t.m % 2, :], xs_t[:, :],
                              keep.w1[:, bass.ds(expert, 1), :].rearrange("p o n -> p (o n)"),
                              start=True, stop=True).then_inc(h_done, 1)
                if t := j.tile(3):
                    pe.wait_ge(h_ready, t.n + 1)
                    wait(pe, ht_ready, t.n - 1)
                    for c in range(CH):
                        mm = pe.transpose(ps[:, 4 + t.m % 2, c * P:(c + 1) * P], h[t.m % 2][:, c * P:(c + 1) * P], w("ident"))
                    mm.then_inc(ht_done, 1)

            run_turns(pe, step, 4, tiles=SLOTS, ahead=2)

        @block.scalar
        def _(act):
            act.wait_ge(best_ready, 1)
            act.activation(shifted[:, :, :], shifted[:, :, :], ACT.Exp).then_inc(exp_ready, 1)

            def step(j):
                if t := j.tile(1):
                    act.wait_ge(xt_done, t.n + 1)
                    wait(act, h_done, t.n)
                    act.activation(xs_t[:, :], ps[:, t.m % 2, 0:P], ACT.Copy).then_inc(xt_ready, 1)
                if t := j.tile(3):
                    act.wait_ge(ht_done, t.n + 1)
                    wait(act, y_done, t.n)
                    act.activation(h_t[:, :, :].rearrange("p c n -> p (c n)"), ps[:, 4 + t.m % 2, :],
                                   ACT.Relu).then_inc(ht_ready, 1)

            run_turns(act, step, 4, tiles=SLOTS, ahead=2)

        @block.vector
        def _(dve):
            chain = Chain(dve, chain_b)
            link = chain.link
            dve.memset(zeros[:, :], 0.0)
            link(dve.tensor_tensor(count[:, :], keep.base[:, :], w("region"), ALU.subtract))
            link(dve.tensor_tensor(fills[:, :, :], spread(count[:, :], 2, TILES), spread(w("tile_rows"), 1, E0), ALU.is_gt))
            link(dve.tensor_reduce(slots[:, :], fills[:, :, :], axis=AX.X, op=ALU.add))
            for k in range(3):
                a, b, by = ends[k - 1] if k else slots[0:1, :], ends[k], 1 << k
                dve.tensor_copy(b[:, 0:by], a[:, 0:by])
                link(dve.tensor_tensor(b[:, by:E0], a[:, by:E0], a[:, 0:E0 - by], ALU.add))
            link(dve.tensor_tensor(past[:, :, :], spread(w("slot_no")[0:1, :], 2, E0), spread(ends[2][:, :], 1, SLOTS), ALU.is_ge))
            link(dve.tensor_reduce(expert_f[:, :], past[:, :, :], axis=AX.X, op=ALU.add))
            link(dve.tensor_tensor(first_row[:, :], slots[0:1, :], ends[2][:, :], ALU.subtract))
            link(dve.scalar_tensor_tensor(first_row[:, :], first_row[:, :], float(P), w("region")[0:1, :], ALU.mult, ALU.add))
            link(dve.tensor_tensor(past[:, :, :], spread(expert_f[:, :], 2, E0), spread(w("expert_no")[0:1, :], 1, SLOTS), ALU.is_equal))
            link(dve.tensor_tensor(past[:, :, :], past[:, :, :], spread(first_row[:, :], 1, SLOTS), ALU.mult))
            link(dve.tensor_reduce(row_f[:, :], past[:, :, :], axis=AX.X, op=ALU.add))
            link(dve.scalar_tensor_tensor(row_f[:, :], w("slot_no")[0:1, :], float(P), row_f[:, :], ALU.mult, ALU.add))
            link(dve.tensor_scalar(unused[:, :], expert_f[:, :], float(E0), float(dummy - ROWS), ALU.is_ge, ALU.mult))
            dve.tensor_tensor(row_i[:, :], row_f[:, :], unused[:, :], ALU.add)
            dve.tensor_scalar(expert_i[:, :], expert_f[:, :], float(E0 - 1), None, ALU.min)
            link(dve.tensor_copy(pad_i[:, :], keep.base[0:1, :]))
            dve.tensor_scalar(count[:, :], count[:, :], 1.0, None, ALU.mult).then_inc(tables_ready, 1)
            dve.tensor_scalar(less[:, :], slots[:, :], -float(P), float(REGION), ALU.mult, ALU.add)
            link(dve.tensor_copy(rows_f[:, :], keep.rows[:, :]))
            link(dve.tensor_tensor(behind[:, :, 1:E0], spread(rows_f[:, :], 2, E0 - 1), spread(w("region")[:, 1:E0], 1, TILES), ALU.is_ge))
            link(dve.tensor_tensor(behind[:, :, 1:E0], behind[:, :, 1:E0], spread(less[:, 0:E0 - 1], 1, TILES), ALU.mult))
            link(dve.tensor_reduce(skipped[:, :], behind[:, :, 1:E0], axis=AX.X, op=ALU.add))
            dve.tensor_tensor(keep.rows[:, :], rows_f[:, :], skipped[:, :], ALU.subtract)
            link(dve.tensor_reduce(best[:, :], keep.logits[:, :, :], axis=AX.X, op=ALU.max))
            dve.tensor_tensor(shifted[:, :, :], keep.logits[:, :, :], spread(best[:, :], 2, E0),
                              ALU.subtract).then_inc(best_ready, 1)
            dve.wait_ge(exp_ready, 1)
            link(dve.tensor_reduce(total[:, :], shifted[:, :, :], axis=AX.X, op=ALU.add))
            dve.reciprocal(keep.prob[:, :], total[:, :])

            def step(j):
                if t := j.tile(2):
                    expert = number(dve, expert_i, t, E0 - 1)
                    dve.wait_ge(h_done, t.n + 1)
                    wait(dve, ht_done, t.n - 1)
                    dve.tensor_tensor(h[t.m % 2][:, :], ps[:, 2 + t.m % 2, :],
                                      keep.b1[:, bass.ds(expert, 1), :].rearrange("p o n -> p (o n)"), ALU.add).then_inc(h_ready, 1)
                if t := j.tile(4):
                    expert = number(dve, expert_i, t, E0 - 1)
                    dve.wait_ge(y_done, t.n + 1)
                    wait(dve, stored[t.m], 16 * t.q)
                    dve.tensor_tensor(y[t.m][:, :], ps[:, 6 + t.m % 2, 0:D],
                                      keep.b2[:, bass.ds(expert, 1), :].rearrange("p o n -> p (o n)"), ALU.add).then_inc(y_ready, 1)

            run_turns(dve, step, 4, tiles=SLOTS, ahead=2)


LINKS_C = 11
C_LAGS = (2, 3, 7)


def layer1(nc, io, keep):
    with ExitStack() as ctx:
        new = lambda name, shape, dt=F32: ctx.enter_context(nc.sbuf_tensor(name, shape, dt))
        sems = lambda name: ctx.enter_context(nc.semaphore(name))
        w = lambda name: WEIGHTS.cols(keep.weights, name)
        ps = ctx.enter_context(nc.psum_tensor("ps_c", [P, 8, 512], F32))

        wvo = new("wvo", [P, D])
        bvo = new("bvo", [P, D])
        bv_wide = new("bv_wide", [P, P])
        head_scaled = new("head_scaled", [P, HALF])
        idx = [new(f"idx{m}", [P, 1], I32) for m in range(2)]
        y = [new(f"y_in{m}", [P, D]) for m in range(2)]
        x2 = [new(f"x2_in{m}", [P, D]) for m in range(2)]
        ctx_t = [new(f"ctx_c{m}", [P, P]) for m in range(UNROLL)]
        x3 = [new(f"x3_{m}", [P, D]) for m in range(2)]
        x3_plus = [new(f"x3_plus{m}", [P, D]) for m in range(2)]
        x4 = [new(f"x4_{m}", [P, D]) for m in range(2)]
        x4_plus = [new(f"x4_plus{m}", [P, D]) for m in range(UNROLL)]
        x5 = [new(f"x5_{m}", [P, D]) for m in range(2)]
        result = [new(f"result{m}", [P, D]) for m in range(2)]
        turned_t = new("turned_c", [P, 3 * P])
        k_t, q_t = new("k_tc", [P, P]), new("q_tc", [P, P])
        v = new("v_c", [P, D])
        sim = new("sim_c", [P, P])
        xk_t = new("xk_t", [P, P])
        xk = new("xk", [P, D])
        xq_t = new("xq_t", [P, P])
        q_heads = new("q_heads", [P, HALF, P])
        e = [new(f"e_c{m}", [P, XH, S]) for m in range(UNROLL)]
        row_max = [new(f"row_max_c{m}", [P, XH]) for m in range(2)]
        rden = new("rden_c", [P, XH])
        rsum = new("rsum_c", [P, XH])
        v_heads = new("v_heads_c", [P, 2, HALF * (HALF * HD + HD)])
        mix_t = new("mix_t", [P, P])
        hid = new("hid", [M1, P])
        hid2 = new("hid2", [M1, P])
        top = [new(f"top_c{m}", [P, 8]) for m in range(UNROLL)]
        norm = Norm(new, sems, "n1", 4)

        x_loaded = [sems(f"xc_loaded{m}") for m in range(2)]
        gathered = [sems(f"gathered{m}") for m in range(2)]
        ctx_loaded = [sems(f"ctx_loaded{m}") for m in range(UNROLL)]
        out_stored = [sems(f"out_stored{m}") for m in range(2)]
        x5_stored = [sems(f"x5_stored{m}") for m in range(2)]
        names = ("idx_ready fused const_ready x3_added x3_ready x3p_ready turned_done turned_ready kq_done kq_ready "
                 "xq_ready side_done xkt_ready hid_relu hid_ready rows_done v_ready xk_ready top_ready gap_ready st_done "
                 "sim_ready sums_done attn_added x4_ready x4p_ready qexp_ready s_done s_read max_ready sub_ready "
                 "e_ready vexp_ready mix_done mix_ready xattn_added x5_ready ffn_added out_ready chain").split()
        (idx_ready, fused, const_ready, x3_added, x3_ready, x3p_ready, turned_done, turned_ready, kq_done, kq_ready,
         xq_ready, side_done, xkt_ready, hid_relu, hid_ready, rows_done, v_ready, xk_ready, top_ready, gap_ready, st_done,
         sim_ready, sums_done, attn_added, x4_ready, x4p_ready, qexp_ready, s_done, s_read, max_ready, sub_ready,
         e_ready, vexp_ready, mix_done, mix_ready, xattn_added, x5_ready, ffn_added, out_ready,
         chain_c) = (sems(n + "_c") for n in names)

        k_ps, q_ps, xq_ps = (ps[:, 0, k * P:(k + 1) * P] for k in range(3))
        v_ps, xk_ps, lg_ps = ps[:, 1, 0:D], ps[:, 1, D:2 * D], ps[:, 1, 2 * D:2 * D + E1]
        st_ps = z_ps = ps[:, 2, 0:P]
        ffn_ps, wo_ps = ps[:, 2, P:2 * P], ps[:, 2, 2 * P:3 * P]
        xkt_ps, hid_ps = ps[:, 6, 0:P], ps[0:M1, 6, P:2 * P]
        s_ps = ps[:, 4:6, :]
        turned_ps = ps[:, 3, 0:3 * P]
        mix_ps = ps[:, 6:8, 2 * P:2 * P + S]

        block = ctx.enter_context(nc.Block())
        LAGS = 7

        def before(j, lag):
            if isinstance(j.n, int):
                return min(max(j.n - lag, 0), TILES)
            return UNROLL * j.q + (j.m - lag)

        def turns(j, lag):
            return max(j.n - lag + 1, 0) if isinstance(j.n, int) else UNROLL * j.q + (j.m - lag + 1)

        @block.sync
        def _(sp):
            def step(j):
                if t := j.tile(0):
                    wait(sp, x3_added, t.n - 1)
                    sp.dma_start(x2[t.m % 2][:, :], plane(io.x2, t.n)).then_inc(x_loaded[t.m % 2], 16)
                if t := j.tile(2):
                    wait(sp, xk_ready, t.n - UNROLL + 1)
                    sp.dma_start(ctx_t[t.m][:, :], plane(io.ctx_p, t.n)).then_inc(ctx_loaded[t.m], 16)
                if t := j.tile(7):
                    sp.wait_ge(x5_ready, t.n + 1)
                    sp.dma_start(plane(io.x5, t.n), x5[t.m % 2][:, :]).then_inc(x5_stored[t.m % 2], 16)
                    sp.wait_ge(out_ready, t.n + 1)
                    sp.dma_start(plane(io.out, t.n), result[t.m % 2][:, :]).then_inc(out_stored[t.m % 2], 16)

            run_turns(sp, step, LAGS)
            for m in range(2):
                sp.wait_ge(out_stored[m], 16 * TILES // 2)
                sp.wait_ge(x5_stored[m], 16 * TILES // 2)

        @block.tensor
        def _(pe):
            pe.wait_ge(const_ready, 1)
            pe.matmul(ps[:, 0, 0:D], w("a1_wv"), w("a1_wo_t"), start=True, stop=True)
            pe.matmul(ps[:, 0, D:2 * D], bv_wide[:, :], w("a1_wo_t"), start=True, stop=True).then_inc(fused, 1)
            pe.wait_ge(const_ready, 2)
            turned = ((2, x3_ready, x3), (3, x4_ready, x4), (7, x5_ready, x5))

            def step(j):
                if t := j.tile(6):
                    pe.wait_ge(vexp_ready, t.n + 1)
                    pe.wait_ge(e_ready, t.n + 1)
                    wait(pe, mix_ready, t.n)
                if t := j.tile(4):
                    pe.wait_ge(qexp_ready, t.n + 1)
                    pe.wait_ge(xkt_ready, t.n + 1)
                    wait(pe, s_read, t.n)
                if t := j.tile(3):
                    pe.wait_ge(ctx_loaded[t.m], 16 * (t.q + 1))
                    wait(pe, hid_relu, before(j, 7))
                    wait(pe, xkt_ready, t.n)
                    mm = pe.matmul(xkt_ps, w("x1_wk"), ctx_t[t.m][:, :], start=True, stop=True)
                    if not j.tile(7):
                        mm.then_inc(side_done, 1)
                if t := j.tile(4):
                    for r in range(2):
                        for b in range(PER):
                            mm = pe.matmul(s_ps[b * S:(b + 1) * S, r, :], xk_t[r * S:(r + 1) * S, b * S:(b + 1) * S],
                                           q_heads[r * S:(r + 1) * S, :, b * S:(b + 1) * S], start=True, stop=True)
                    mm.then_inc(s_done, 1)
                if t := j.tile(6):
                    for h in range(HALF):
                        for half in range(2):
                            for b in range(PER):
                                rows = slice(b * S, (b + 1) * S)
                                mm = pe.matmul(mix_ps[half * S:(half + 1) * S, b, :],
                                               v_heads[rows, half, h * HALF * HD:(h + 1) * HALF * HD],
                                               e[t.m][rows, half * HALF + h, :], start=(h == 0), stop=(h == HALF - 1))
                    mm.then_inc(mix_done, 1)
                wait(pe, turned_ready, turns(j, 2) - 1)
                for k, (lag, ready, src) in enumerate(turned):
                    if t := j.tile(lag):
                        pe.wait_ge(ready, t.n + 1)
                        pe.transpose(turned_ps[:, k * P:(k + 1) * P], src[t.m % 2][:, :], w("ident")).then_inc(turned_done, 1)
                wait(pe, xk_ready, before(j, 5))
                wait(pe, v_ready, before(j, 2))
                wait(pe, top_ready, before(j, 7))
                if t := j.tile(5):
                    mm_rows = pe.matmul(xk_ps, ctx_t[t.m][:, :], w("x1_wk"), start=True, stop=True)
                if j.tile(2) or j.tile(3) or j.tile(7):
                    pe.wait_ge(turned_ready, turns(j, 2))
                if j.tile(2) or j.tile(3):
                    wait(pe, kq_ready, before(j, 2))
                    wait(pe, xq_ready, before(j, 3))
                if t := j.tile(2):
                    pe.matmul(k_ps, w("a1_wk_t"), turned_t[:, 0:P], start=True, stop=True)
                    mm = pe.matmul(q_ps, w("a1_wq_t"), turned_t[:, 0:P], start=True, stop=True)
                if t := j.tile(3):
                    mm = pe.matmul(xq_ps, w("x1_wq"), turned_t[:, P:2 * P], start=True, stop=True)
                if j.tile(2) or j.tile(3):
                    mm.then_inc(kq_done, 1)
                wait(pe, mix_ready, before(j, 6) if not j.tile(6) else j.tile(6).n + 1)
                if t := j.tile(7):
                    mm_side = pe.matmul(hid_ps, w("shared_w1"), turned_t[:, 2 * P:3 * P], start=True, stop=True)
                    mm_side.then_inc(side_done, 1)
                if t := j.tile(2):
                    mm_rows = pe.matmul(v_ps, turned_t[:, 0:P], wvo[:, :], start=True, stop=True)
                if t := j.tile(7):
                    mm_rows = pe.matmul(lg_ps, turned_t[:, 2 * P:3 * P], w("route_w"), start=True, stop=True)
                if j.tile(2) or j.tile(5) or j.tile(7):
                    mm_rows.then_inc(rows_done, 1)
                wait(pe, attn_added, before(j, 2))
                wait(pe, xattn_added, before(j, 6))
                wait(pe, ffn_added, before(j, 7))
                if t := j.tile(2):
                    pe.wait_ge(kq_ready, t.n + 1)
                    pe.matmul(st_ps, k_t[:, :], q_t[:, :], start=True, stop=True).then_inc(st_done, 1)
                if t := j.tile(2):
                    pe.wait_ge(sim_ready, t.n + 1)
                    pe.wait_ge(v_ready, t.n + 1)
                    mm = pe.matmul(z_ps, sim[:, :], v[:, :], start=True, stop=True)
                if t := j.tile(6):
                    pe.wait_ge(mix_ready, t.n + 1)
                    mm = pe.matmul(wo_ps, mix_t[:, :], w("x1_wo"), start=True, stop=True)
                if t := j.tile(7):
                    pe.wait_ge(hid_ready, t.n + 1)
                    mm = pe.matmul(ffn_ps, hid2[:, :], w("shared_w2")[0:M1, :], start=True, stop=True)
                if j.tile(2) or j.tile(6) or j.tile(7):
                    mm.then_inc(sums_done, 1)

            run_turns(pe, step, LAGS)

        @block.scalar
        def _(act):
            def step(j):
                if t := j.tile(4):
                    act.wait_ge(s_done, t.n + 1)
                    wait(act, mix_done, t.n - UNROLL + 1)
                    act.activation(e[t.m][:, :, :].rearrange("p h n -> p (h n)"), s_ps.rearrange("p r n -> p (r n)"),
                                   ACT.Copy).then_inc(s_read, 1)
                if t := j.tile(6):
                    act.wait_ge(mix_done, t.n + 1)
                    wait(act, sums_done, turns(j, 2) - 1)
                    act.activation(mix_t[:, :].rearrange("p (b n) -> p b n", b=PER), mix_ps, ACT.Copy).then_inc(mix_ready, 1)
                here = [k for k, lag in enumerate(C_LAGS) if j.tile(lag)]
                if here:
                    act.wait_ge(turned_done, turned_count(j, C_LAGS))
                    r = slice(here[0] * P, (here[-1] + 1) * P)
                    act.activation(turned_t[:, r], turned_ps[:, r], ACT.Copy).then_inc(turned_ready, 1)
                if t := j.tile(5):
                    act.wait_ge(sub_ready, t.n + 1)
                    act.activation(e[t.m][:, :, :], e[t.m][:, :, :], ACT.Exp).then_inc(e_ready, 1)
                if j.tile(2) or j.tile(3):
                    act.wait_ge(kq_done, turns(j, 2))
                if t := j.tile(2):
                    wait(act, st_done, t.n)
                    act.activation(k_t[:, :], k_ps, ACT.Identity, bias=w("a1_bk"))
                    act.activation(q_t[:, :], q_ps, ACT.Identity, bias=w("a1_bq")).then_inc(kq_ready, 1)
                if t := j.tile(3):
                    wait(act, qexp_ready, t.n)
                    act.activation(xq_t[:, :], xq_ps, ACT.Identity, bias=w("x1_bq")).then_inc(xq_ready, 1)
                if t := j.tile(7):
                    act.wait_ge(side_done, turns(j, 3))
                    act.activation(hid[:, :], hid_ps, ACT.Relu).then_inc(hid_relu, 1)
                if t := j.tile(3):
                    if not j.tile(7):
                        act.wait_ge(side_done, turns(j, 3))
                    wait(act, s_done, t.n)
                    act.activation(xk_t[:, :], xkt_ps, ACT.Identity, bias=w("x1_bk")).then_inc(xkt_ready, 1)
                if t := j.tile(7):
                    act.wait_ge(hid_relu, t.n + 1)
                    wait(act, sums_done, turns(j, 2) - 1)
                    act.activation(hid2[:, :], hid[:, :], ACT.Square).then_inc(hid_ready, 1)
                lanes = [k for k, lag in enumerate((1, 2, 6, 7)) if j.tile(lag)]
                if lanes:
                    norm_scalar(act, norm, j.n, lanes[0], lanes[-1] + 1)

            run_turns(act, step, LAGS)

        @block.gpsimd
        def _(pool):
            pool.wait_ge(const_ready, 1)

            def step(j):
                if t := j.tile(0):
                    pool.wait_ge(idx_ready, t.n + 1)
                    wait(pool, x3_added, t.n - 1)
                if t := j.tile(5):
                    pool.wait_ge(max_ready, t.n + 1)
                    pool.tensor_tensor(e[t.m][:, :, :], e[t.m][:, :, :], spread(row_max[t.m % 2][:, :], 2, S),
                                       ALU.subtract).then_inc(sub_ready, 1)
                if t := j.tile(0):
                    pool.indirect_dma_start(y[t.m % 2][:, :], None, io.y,
                                            bass.IndirectOffsetOnAxis(ap=idx[t.m % 2][:, 0:1], axis=0)).then_inc(gathered[t.m % 2], 16)
                if t := j.tile(2):
                    pool.wait_ge(x3_ready, t.n + 1)
                    wait(pool, attn_added, t.n - 1)
                    pool.tensor_tensor(x3_plus[t.m % 2][:, :], x3[t.m % 2][:, :], w("a1_bo"), ALU.add).then_inc(x3p_ready, 1)
                if t := j.tile(3):
                    pool.wait_ge(x4_ready, t.n + 1)
                    wait(pool, xattn_added, t.n - UNROLL + 1)
                    pool.tensor_tensor(x4_plus[t.m][:, :], x4[t.m % 2][:, :], w("x1_bo"), ALU.add).then_inc(x4p_ready, 1)
                    pool.wait_ge(xq_ready, t.n + 1)
                    wait(pool, s_done, t.n)
                    pool.tensor_tensor(q_heads[:, :, :], spread(xq_t[:, :], 1, HALF), spread(head_scaled[:, :], 2, P),
                                       ALU.mult).then_inc(qexp_ready, 1)
                if t := j.tile(7):
                    pool.wait_ge(top_ready, t.n + 1)
                    pool.tensor_tensor(pick(keep.gap, t), top[t.m][:, 0:1], top[t.m][:, 1:2],
                                       ALU.subtract).then_inc(gap_ready, 1)

            run_turns(pool, step, LAGS)

        @block.vector
        def _(dve):
            chain = Chain(dve, chain_c)
            dve.memset(v_heads[:, :, :], 0.0)
            dve.memset(norm.idle[:, :], 0.0)
            dve.tensor_copy(bv_wide[:, :], w("a1_bv").broadcast_to([P, P]))
            dve.tensor_scalar(head_scaled[:, :], w("head_of_row"), HD ** -0.5, None, ALU.mult).then_inc(const_ready, 1)
            dve.wait_ge(fused, 1)
            dve.tensor_copy(wvo[:, :], ps[:, 0, 0:D])
            chain.link(dve.tensor_copy(bvo[:, :], ps[:, 0, D:2 * D]))
            dve.tensor_copy(norm.idle[:, 0:1], norm.idle[:, 1:2]).then_inc(const_ready, 1)

            def step(j):
                if t := j.tile(0):
                    wait(dve, gathered[t.m % 2], 32 * t.q + 16 * (t.m // 2))
                    dve.tensor_copy(idx[t.m % 2][:, :], pick(keep.rows, t)).then_inc(idx_ready, 1)
                if t := j.tile(4):
                    dve.wait_ge(s_read, t.n + 1)
                    wait(dve, sub_ready, t.n - 1)
                    dve.tensor_reduce(row_max[t.m % 2][:, :], e[t.m][:, :, :], axis=AX.X, op=ALU.max).then_inc(max_ready, 1)
                if j.tile(2) or j.tile(5) or j.tile(7):
                    dve.wait_ge(rows_done, turns(j, 2))
                    if t := j.tile(7):
                        wait(dve, gap_ready, t.n - 1)
                if t := j.tile(2):
                    wait(dve, sums_done, before(j, 2))
                    dve.tensor_tensor(v[:, :], v_ps, bvo[:, :], ALU.add).then_inc(v_ready, 1)
                if t := j.tile(5):
                    with_bias = chain.mark(dve.tensor_tensor(xk[:, :], xk_ps, w("x1_bk_row"), ALU.add))
                    dve.tensor_copy(norm.idle[:, 0:1], norm.idle[:, 1:2]).then_inc(xk_ready, 1)
                if t := j.tile(7):
                    dve.max(out=top[t.m][:, :], in_=lg_ps).then_inc(top_ready, 1)
                if t := j.tile(2):
                    dve.wait_ge(st_done, t.n + 1)
                    dve.tensor_tensor(sim[:, :], st_ps, w("decay"), ALU.mult).then_inc(sim_ready, 1)
                if t := j.tile(5):
                    dve.wait_ge(e_ready, t.n + 1)
                    chain.link(dve.tensor_reduce(rsum[:, :], e[t.m][:, :, :], axis=AX.X, op=ALU.add))
                    chain.link(dve.reciprocal(rden[:, :], rsum[:, :]))
                    chain.wait(with_bias)
                    wait(dve, mix_done, t.n)
                    dve.tensor_tensor(v_heads[:, :, :].rearrange("p g (h n) -> p g h n", h=HALF)[:, :, :, 0:HD],
                                      xk[:, :].rearrange("p (g h n) -> p g h n", g=2, h=HALF),
                                      spread(rden[:, :].rearrange("p (g h) -> p g h", g=2), 3, HD),
                                      ALU.mult).then_inc(vexp_ready, 1)
                lanes = []
                if t := j.tile(1):
                    dve.wait_ge(x_loaded[t.m % 2], 32 * t.q + 16 * (t.m // 2 + 1))
                    dve.wait_ge(gathered[t.m % 2], 32 * t.q + 16 * (t.m // 2 + 1))
                    dve.scalar_tensor_tensor(norm.sum[0][:, :], y[t.m % 2][:, :], pick(keep.prob, t), x2[t.m % 2][:, :],
                                             ALU.mult, ALU.add).then_inc(x3_added, 1)
                    lanes.append((0, x3[t.m % 2][:, :], x3_ready, lambda t=t: wait(dve, x3p_ready, t.n - 1)))
                if j.tile(2) or j.tile(6) or j.tile(7):
                    dve.wait_ge(sums_done, turns(j, 2))
                if t := j.tile(2):
                    dve.wait_ge(x3p_ready, t.n + 1)
                    dve.tensor_tensor(norm.sum[1][:, :], z_ps, x3_plus[t.m % 2][:, :], ALU.add).then_inc(attn_added, 1)
                    lanes.append((1, x4[t.m % 2][:, :], x4_ready, lambda t=t: wait(dve, x4p_ready, t.n - 1)))
                if t := j.tile(6):
                    dve.wait_ge(x4p_ready, t.n + 1)
                    dve.tensor_tensor(norm.sum[2][:, :], wo_ps, x4_plus[t.m][:, :], ALU.add).then_inc(xattn_added, 1)
                    lanes.append((2, x5[t.m % 2][:, :], x5_ready,
                                  lambda t=t: wait(dve, x5_stored[t.m % 2], 32 * t.q + 16 * (t.m // 2))))
                if t := j.tile(7):
                    dve.wait_ge(x5_ready, t.n + 1)
                    wait(dve, out_ready, t.n)
                    dve.tensor_tensor(norm.sum[3][:, :], ffn_ps, x5[t.m % 2][:, :], ALU.add).then_inc(ffn_added, 1)
                    lanes.append((3, result[t.m % 2][:, :], out_ready,
                                  lambda t=t: wait(dve, out_stored[t.m % 2], 32 * t.q + 16 * (t.m // 2))))
                for lag, sem in ((1, x3_added), (2, attn_added), (6, xattn_added), (7, ffn_added)):
                    if t := j.tile(lag):
                        dve.wait_ge(sem, t.n + 1)
                if lanes:
                    norm_vector(dve, chain, norm, j.n, lanes)

            run_turns(dve, step, LAGS, chain, LINKS_C)


GAP = 16.0
LINKS_D = 17


def layer1_routed(nc, io, keep):
    with ExitStack() as ctx:
        new = lambda name, shape, dt=F32: ctx.enter_context(nc.sbuf_tensor(name, shape, dt))
        sems = lambda name: ctx.enter_context(nc.semaphore(name))
        w = lambda name: WEIGHTS.cols(keep.weights, name)
        ps = ctx.enter_context(nc.psum_tensor("ps_d", [P, 8, 512], F32))
        pairs = E1 // 2

        gap_max = new("gap_max", [P, 1])
        all_max = new("all_max", [1, 1])
        flag = new("flag", [1, 1], I32)
        w1, w2 = new("w1_d", [P, E1 * M1]), new("w2_d", [P, pairs, D])
        x5, x5_t = new("x5_d", [P, D]), new("x5_td", [P, P])
        hid, hid2 = new("hid_d", [P, pairs, P]), new("hid2_d", [P, pairs, P])
        own, own2 = new("own_d", [M1, P]), new("own2_d", [M1, P])
        lg, top, top_at, top_f = new("lg_d", [P, E1]), new("top_d", [P, 8]), new("top_at_d", [P, 8], U32), new("top_fd", [P, 1])
        gap, other = new("gap_d", [P, 1]), new("other_d", [P, 1])
        kept, chosen = new("kept_d", [P, 1]), new("chosen_d", [P, E1])
        result = new("result_d", [P, D])
        norm = Norm(new, sems, "n2", 1)

        (gap_ready, max_turned, flag_ready, loaded, turned_done, turned_ready, hid_done, hid_ready, squared, gap2_ready,
         exp_ready, y_done, added, out_ready, stored, chain_d) = (sems(n + "_d") for n in (
             "gap_ready", "max_turned", "flag_ready", "loaded", "turned_done", "turned_ready", "hid_done",
             "hid_ready", "squared", "gap2_ready", "exp_ready", "y_done", "added", "out_ready", "stored", "chain"))
        hid_ps = ps[:, 1, :]
        own_ps = ps[0:M1, 2, 0:P]
        lg_ps = ps[:, 3, 0:E1]
        shared_ps = ps[:, 6, 0:D]

        block = ctx.enter_context(nc.Block())

        def needed(eng):
            eng.wait_ge(flag_ready, 1)
            return eng.value_load(flag[0:1, 0:1], min_val=0, max_val=1) > 0

        @block.sync
        def _(sp):
            with sp.If(needed(sp)):
                sp.dma_start(w1[:, :], io.routed_w1).then_inc(loaded, 16)
                sp.dma_start(w2[:, :, :].rearrange("p c n -> p (c n)"), io.routed_w2).then_inc(loaded, 16)
                sp.wait_ge(loaded, 32)
                with sp.Fori(0, TILES) as i:
                    sp.wait_ge(added, i)
                    sp.dma_start(x5[:, :], plane(io.x5, i)).then_inc(loaded, 16)
                    sp.wait_ge(out_ready, i + 1)
                    sp.dma_start(plane(io.out, i), result[:, :]).then_inc(stored, 16)
                sp.wait_ge(stored, 16 * TILES)

        @block.tensor
        def _(pe):
            pe.wait_ge(gap_ready, 1)
            pe.transpose(ps[0:1, 7, 0:P], gap_max[:, :], w("ident")).then_inc(max_turned, 1)
            with pe.If(needed(pe)):
                with pe.Fori(0, TILES) as i:
                    pe.wait_ge(loaded, i * 16 + 48)
                    pe.transpose(ps[:, 0, 0:P], x5[:, :], w("ident")).then_inc(turned_done, 1)
                    pe.wait_ge(turned_ready, i + 1)
                    pe.matmul(lg_ps, x5_t[:, :], w("route_w"), start=True, stop=True)
                    for c in range(pairs):
                        pe.matmul(hid_ps[:, c * P:(c + 1) * P], w1[:, c * P:(c + 1) * P], x5_t[:, :], start=True, stop=True)
                    pe.matmul(own_ps, w("shared_w1"), x5_t[:, :], start=True, stop=True).then_inc(hid_done, 1)
                    pe.wait_ge(squared, i + 1)
                    pe.matmul(shared_ps, own2[:, :], w("shared_w2")[0:M1, :], start=True, stop=True)
                    for c in range(pairs):
                        for k in range(2):
                            rows = slice(k * M1, (k + 1) * M1)
                            mm = pe.matmul(ps[:, 4 + k, c * D:(c + 1) * D], hid2[rows, c, :], w2[rows, c, :], start=True, stop=True)
                    mm.then_inc(y_done, 1)

        @block.scalar
        def _(act):
            with act.If(needed(act)):
                with act.Fori(0, TILES) as i:
                    act.wait_ge(turned_done, i + 1)
                    act.activation(x5_t[:, :], ps[:, 0, 0:P], ACT.Copy).then_inc(turned_ready, 1)
                    act.wait_ge(hid_done, i + 1)
                    act.activation(hid[:, :, :].rearrange("p c n -> p (c n)"), hid_ps, ACT.Relu)
                    act.activation(own[:, :], own_ps, ACT.Relu).then_inc(hid_ready, 1)
                    act.wait_ge(gap2_ready, i + 1)
                    act.activation(other[:, :], gap[:, :], ACT.Exp).then_inc(exp_ready, 1)
                    norm_scalar(act, norm, i + 1, 0, 1)

        @block.vector
        def _(dve):
            chain = Chain(dve, chain_d)
            chain.link(dve.memset(norm.idle[:, :], 0.0))
            dve.tensor_reduce(gap_max[:, :], keep.gap[:, :], axis=AX.X, op=ALU.max).then_inc(gap_ready, 1)
            dve.wait_ge(max_turned, 1)
            chain.link(dve.tensor_reduce(all_max[:, :], ps[0:1, 7, 0:P], axis=AX.X, op=ALU.max))
            dve.tensor_scalar(flag[:, :], all_max[:, :], GAP, None, ALU.is_gt).then_inc(flag_ready, 1)
            with dve.If(needed(dve)):
                before = chain.count
                with dve.Fori(0, TILES) as i:
                    chain.turn = (i, LINKS_D, 0)
                    dve.wait_ge(hid_done, i + 1)
                    chain.link(dve.tensor_copy(lg[:, :], lg_ps))
                    dve.tensor_copy(norm.idle[:, 0:1], norm.idle[:, 1:2])
                    chain.link(dve.max(out=top[:, :], in_=lg[:, :]))
                    dve.tensor_tensor(gap[:, :], top[:, 1:2], top[:, 0:1], ALU.subtract).then_inc(gap2_ready, 1)
                    chain.link(dve.max_index(out=top_at[:, :], in_max=top[:, :], in_values=lg[:, :]))
                    dve.tensor_copy(top_f[:, :], top_at[:, 0:1])
                    dve.wait_ge(exp_ready, i + 1)
                    dve.tensor_scalar(kept[:, :], other[:, :], 1.0, 1.0, ALU.add, ALU.is_le)
                    chain.link(dve.tensor_copy(norm.idle[:, 0:1], norm.idle[:, 1:2]))
                    dve.tensor_scalar(chosen[:, :], w("expert_no"), top_f[:, 0:1], kept[:, 0:1], ALU.is_equal, ALU.mult)
                    dve.wait_ge(hid_ready, i + 1)
                    dve.tensor_tensor(hid2[:, :, :], hid[:, :, :], hid[:, :, :], ALU.mult)
                    dve.tensor_tensor(own2[:, :], own[:, :], own[:, :], ALU.mult).then_inc(squared, 1)
                    dve.wait_ge(y_done, i + 1)
                    dve.wait_ge(loaded, i * 16 + 48)
                    dve.tensor_tensor(norm.sum[0][:, :], shared_ps, x5[:, :], ALU.add).then_inc(added, 1)
                    dve.wait_ge(added, i + 1)
                    for k in range(E1):
                        chain.link(dve.scalar_tensor_tensor(norm.sum[0][:, :], ps[:, 4 + k % 2, k // 2 * D:(k // 2 + 1) * D],
                                                            chosen[:, k:k + 1], norm.sum[0][:, :], ALU.mult, ALU.add))
                    norm_vector(dve, chain, norm, i + 1, [(0, result[:, :], out_ready, lambda: dve.wait_ge(stored, i * 16))])
                assert chain.count == before + LINKS_D, chain.count - before


def lay_out(inputs):
    f = {k: np.asarray(v) for k, v in inputs.items()}
    row = lambda a: np.broadcast_to(a.reshape(1, -1), (P, a.size))
    col = lambda a: a.reshape(P, 1)
    head_major = lambda a: a.transpose(1, 0, 2).reshape(P, -1)
    p, s, c = np.arange(P), np.arange(S), HALF // 2
    const = {
        "ident": np.eye(P), "causal": (s[None] >= p[:, None] % S) / S,
        "head_of_row": p[:, None] % S // HD == np.arange(HALF),
        "expert_no": np.broadcast_to(np.arange(E0), (P, E0)), "region": np.broadcast_to(np.arange(E0) * REGION, (P, E0)),
        "before": p[:, None] < p[None],
        "tile_rows": np.broadcast_to(np.arange(TILES) * P, (P, TILES)), "slot_no": np.broadcast_to(np.arange(SLOTS), (P, SLOTS)),
        "ones_at": (np.arange(HALF)[None, None] == 2 * np.arange(c)[None, :, None] + (p // S)[:, None, None]).reshape(P, -1),
        "decay": np.where((p[:, None] < p[None]) & (p[:, None] // S == p[None] // S),
                          0.01 * 0.99 ** np.maximum(p[None] - p[:, None] - 1, 0).astype(np.float64), 0.0),
    }
    kv = f["L0_xattn_W_kv"].reshape(D, XH, 2, HD)
    b_kv = f["L0_xattn_b_kv"].reshape(XH, 2, HD)
    w2s = np.zeros((P, D), np.float32)
    w2s[:M1] = f["L1_ffn_Ws2"]
    parts = {
        "wq_heads": head_major(f["L0_attn_Wq"]), "wk_heads": head_major(f["L0_attn_Wk"]),
        "wv_t": f["L0_attn_Wv"].transpose(2, 0, 1).reshape(D, -1),
        "x0_wk": kv[:, :, 0].reshape(D, D), "x0_wv": kv[:, :, 1].reshape(D, D), "x0_wq": f["L0_xattn_W_q"],
        "x0_wo": f["L0_xattn_W_o"], "x0_bk": col(b_kv[:, 0]), "x0_bq": col(f["L0_xattn_b_q"]),
        "x0_bv": row(np.tile(b_kv[:, 1].reshape(-1), PER)), "x0_bo": row(f["L0_xattn_b_o"]),
        "gate_w": f["L0_ffn_w_gate"], "gate_b": row(f["L0_ffn_b_gate"]),
        "a1_wk_t": f["L1_attn_Wk"].T, "a1_wq_t": f["L1_attn_Wq"].T, "a1_wv": f["L1_attn_Wv"], "a1_wo_t": f["L1_attn_Wo"].T,
        "a1_bk": col(f["L1_attn_bk"]), "a1_bq": col(f["L1_attn_bq"]), "a1_bv": col(f["L1_attn_bv"]),
        "a1_bo": row(f["L1_attn_bo"]),
        "x1_wq": f["L1_xattn_Wq"], "x1_wk": f["L1_xattn_Wk"], "x1_wo": f["L1_xattn_Wo"], "x1_bq": col(f["L1_xattn_bq"]),
        "x1_bk": col(f["L1_xattn_bk"]), "x1_bk_row": row(f["L1_xattn_bk"]), "x1_bo": row(f["L1_xattn_bo"]),
        "shared_w1": f["L1_ffn_Ws1"], "shared_w2": w2s, "route_w": f["L1_ffn_Wr"],
    }
    blob = lambda b: np.concatenate([np.asarray({**parts, **const}[n], np.float32).reshape(P, -1) for n in b.at], axis=1)
    ctx = f["ctx_1024"].reshape(TILES, PER, S, D).transpose(0, 3, 1, 2)
    tokens = f["x"].reshape(TILES, P, D)
    return {
        "first": blob(FIRST), "weights": blob(WEIGHTS), "x": tokens, "x_t": np.ascontiguousarray(tokens.transpose(0, 2, 1)),
        "ctx_t": np.ascontiguousarray(np.broadcast_to(ctx[:, :, :, None], (TILES, D, PER, 2, S))).reshape(TILES, D, -1),
        "ctx_p": np.ascontiguousarray(ctx).reshape(TILES, D, P),
        "mask": np.ascontiguousarray(f["mask_BxSxS2_ik0"].reshape(TILES, P, S).transpose(1, 0, 2)),
        "routed_w1": np.ascontiguousarray(f["L1_ffn_W1"].transpose(1, 0, 2)).reshape(D, -1),
        "routed_w2": np.ascontiguousarray(f["L1_ffn_W2"].reshape(E1 // 2, P, D).transpose(1, 0, 2)).reshape(P, -1),
        "w1": np.ascontiguousarray(f["L0_ffn_W1"].transpose(1, 0, 2)),
        "w2": np.ascontiguousarray(f["L0_ffn_W2"].reshape(E0, CH, P, D).transpose(2, 0, 1, 3)),
        "b1": np.ascontiguousarray(np.broadcast_to(f["L0_ffn_b1"][None], (P, E0, M0))),
        "b2": np.ascontiguousarray(np.broadcast_to(f["L0_ffn_b2"][None], (P, E0, D))),
    }


def build(nc, io):
    with ExitStack() as ctx:
        new = lambda name, shape, dt=F32: ctx.enter_context(nc.sbuf_tensor(name, shape, dt))
        keep = Kept()
        keep.weights = new("weights", [P, WEIGHTS.width])
        keep.rows = new("rows", [P, TILES], I32)
        keep.logits = new("logits", [P, TILES, E0])
        keep.base = new("base", [P, E0])
        keep.prob = new("prob", [P, TILES])
        keep.gap = new("gap", [P, TILES])
        keep.ffn_loaded = ctx.enter_context(nc.semaphore("ffn_loaded"))
        with ExitStack() as experts:
            own = lambda name, shape: experts.enter_context(nc.sbuf_tensor(name, shape, F32))
            keep.w1, keep.w2 = own("w1", [P, E0, M0]), own("w2", [P, E0, CH, D])
            keep.b1, keep.b2 = own("b1", [P, E0, M0]), own("b2", [P, E0, D])
            layer0_attention(nc, io, keep)
            layer0_experts(nc, io, keep)
        layer1(nc, io, keep)
        layer1_routed(nc, io, keep)


def kernel(**inputs):
    import concourse.bacc as _bacc
    from concourse.bass_utils import run_bass_kernel_spmd as _run

    nc = _bacc.Bacc("TRN2", target_bir_lowering=False, num_devices=1)
    laid = lay_out(inputs)
    io = Arrays()
    put = vars(io)
    for name, a in laid.items():
        put[name] = nc.dram_tensor(f"in_{name}", a.shape, mybir.dt.from_np(a.dtype), kind="ExternalInput").ap()
    for name, shape in (("x2", (TILES, P, D)), ("sorted", (E0 * REGION + (SLOTS - TILES) * P, D)),
                        ("y", (SLOTS * P, D)), ("x5", (TILES, P, D))):
        put[name] = nc.dram_tensor(f"mid_{name}", shape, F32, kind="Internal").ap()
    put["out"] = nc.dram_tensor("out_0", (TILES, P, D), F32, kind="ExternalOutput").ap()
    build(nc, io)
    r = _run(nc, [{f"in_{name}": a for name, a in laid.items()}], core_ids=[0])
    return r.results[0]["out_0"].reshape(B, S, D)
```

```python
from contextlib import ExitStack

import numpy as np
import concourse.bass as bass
from concourse import mybir

F32 = mybir.dt.float32
BF16 = mybir.dt.bfloat16
I32 = mybir.dt.int32
U32 = mybir.dt.uint32
ALU = mybir.AluOpType
ACT = mybir.ActivationFunctionType
AX = mybir.AxisListType

B, S, D = 64, 64, 128
P = 128
TILES = B * S // P
PER = P // S
AH = 8
XH, HD = 16, 8
HALF = XH // 2
E0, M0 = 8, 512
CH = M0 // P
E1, M1 = 8, 64
EPS = 1e-5
ROWS = B * S
REGION = ROWS + P
UNROLL = 4
SLOTS = -(-(ROWS // P + E0 - 1) // UNROLL) * UNROLL
VW = HALF * HD + HALF


class Blob:

    def __init__(self, parts):
        self.at, self.width = {}, 0
        for name, n in parts:
            self.at[name] = (self.width, n)
            self.width += n

    def cols(self, ap, name):
        at, n = self.at[name]
        return ap[:, at:at + n]


FIRST = Blob([("wq_heads", AH * D), ("wk_heads", AH * D)])
WEIGHTS = Blob([
    ("ident", P), ("wv_t", AH * D), ("causal", S), ("head_of_row", HALF), ("expert_no", E0), ("region", E0), ("before", P),
    ("tile_rows", TILES), ("slot_no", SLOTS),
    ("ones_at", HALF // 2 * HALF),
    ("x0_wk", D), ("x0_wv", D), ("x0_wq", D), ("x0_wo", D), ("x0_bk", 1), ("x0_bq", 1), ("x0_bv", PER * D), ("x0_bo", D),
    ("gate_w", E0), ("gate_b", E0),
    ("a1_wk_t", D), ("a1_wq_t", D), ("a1_wv", D), ("a1_wo_t", D), ("a1_bk", 1), ("a1_bq", 1), ("a1_bv", 1), ("a1_bo", D),
    ("decay", P),
    ("x1_wq", D), ("x1_wk", D), ("x1_wo", D), ("x1_bq", 2), ("x1_bk", 2), ("x1_bk_row", D), ("x1_bo", D),
    ("shared_w1", M1), ("shared_w2", D), ("route_w", E1),
])


class Arrays:
    pass


class Kept:
    pass


class Tile:

    def __init__(self, q, m):
        self.q, self.m = q, m
        self.n = UNROLL * q + m


class Turn:

    def __init__(self, q, m, tiles=TILES):
        self.q, self.m, self.tiles = q, m, tiles
        self.n = UNROLL * q + m

    def tile(self, lag):
        up, m = divmod(self.m - lag, UNROLL)
        if isinstance(self.q, int) and not 0 <= self.n - lag < self.tiles:
            return None
        return Tile(self.q + up, m)


def wait(eng, sem, value):
    if isinstance(value, int) and value <= 0:
        return
    eng.wait_ge(sem, value)


class Chain:

    def __init__(self, eng, sem):
        self.eng, self.sem, self.count, self.turn = eng, sem, 0, None

    def mark(self, instruction):
        instruction.then_inc(self.sem, 1)
        self.count += 1
        return self.count

    def wait(self, mark):
        if self.turn is None:
            self.eng.wait_ge(self.sem, mark)
        else:
            i, per, less = self.turn
            self.eng.wait_ge(self.sem, i * per + (mark - less))

    def link(self, instruction):
        self.wait(self.mark(instruction))


def run_turns(eng, step, lags, chain=None, links=0, tiles=TILES, ahead=0):
    first, last = -(-(lags + ahead) // UNROLL), tiles // UNROLL
    for n in range(UNROLL * first):
        step(Turn(*divmod(n, UNROLL), tiles))
    before = chain.count if chain else 0
    with eng.Fori(first, last) as i:
        if chain:
            chain.turn = (i, UNROLL * links, UNROLL * links * first)
        for m in range(UNROLL):
            step(Turn(i, m, tiles))
    if chain:
        assert chain.count == before + UNROLL * links, (chain.count - before) / UNROLL
        chain.turn, chain.count = None, before + UNROLL * links * (last - first)
    for n in range(UNROLL * last, tiles + lags):
        step(Turn(*divmod(n, UNROLL), tiles))


def split_heads(ap):
    return ap.rearrange("p (h n) -> p h n", h=HALF)


def spread(ap, axis, n):
    names = ["p", "a", "b"][:len(ap.shape)]
    to = names[:axis] + ["o"] + names[axis:]
    merged = names[:axis] + ["(o " + names[axis] + ")"] + names[axis + 1:] if axis < len(names) else names[:-1] + ["(" + names[-1] + " o)"]
    shape = list(ap.shape)
    return ap.rearrange(" ".join(merged) + " -> " + " ".join(to), o=1).broadcast_to(shape[:axis] + [n] + shape[axis:])


class Norm:

    def __init__(self, new, sems, name, lanes):
        self.sum = [new(f"{name}_sum{k}", [P, D]) for k in range(lanes)]
        self.stats = new(f"{name}_stats", [P, lanes, 6])
        self.moments = new(f"{name}_moments", [P, lanes, 2])
        self.var = new(f"{name}_var", [P, lanes])
        self.log = new(f"{name}_log", [P, lanes])
        self.guess = new(f"{name}_guess", [P, lanes])
        self.half = new(f"{name}_half", [P, lanes])
        self.rstd = new(f"{name}_rstd", [P, lanes])
        self.idle = new(f"{name}_idle", [P, 2])
        self.var_ready, self.guess_ready, self.log_ready = (sems(f"{name}_{x}") for x in ("var_ready", "guess_ready", "log_ready"))


def norm_scalar(act, norm, count, a, b):
    act.wait_ge(norm.var_ready, count)
    act.activation(norm.log[:, a:b], norm.var[:, a:b], ACT.Ln).then_inc(norm.log_ready, 1)
    act.wait_ge(norm.log_ready, count)
    act.activation(norm.guess[:, a:b], norm.log[:, a:b], ACT.Exp, scale=-0.5).then_inc(norm.guess_ready, 1)


def norm_vector(dve, chain, norm, count, lanes, counted=(), summed={}, meanwhile=lambda: None):
    ks = [lane[0] for lane in lanes]
    a, b = min(ks), max(ks) + 1
    for k in ks:
        if k not in counted:
            if k in summed:
                dve.wait_ge(*summed[k])
            last = dve.bn_stats(norm.stats[:, k, :], norm.sum[k][:, :])
    if all(k in counted for k in ks):
        last = dve.tensor_copy(norm.idle[:, 0:1], norm.idle[:, 1:2])
    chain.link(last)
    dve.tensor_copy(norm.idle[:, 0:1], norm.idle[:, 1:2])
    for k in ks:
        last = chain.mark(dve.bn_aggr(norm.moments[:, k, :], norm.stats[:, k, :]))
    chain.wait(last)
    dve.tensor_scalar(norm.var[:, a:b], norm.moments[:, a:b, 1], EPS, None, ALU.add).then_inc(norm.var_ready, 1)
    meanwhile()
    dve.wait_ge(norm.guess_ready, count)
    guess = norm.guess[:, a:b]
    chain.link(dve.scalar_tensor_tensor(norm.half[:, a:b], guess, -0.5, guess, ALU.mult, ALU.mult))
    chain.link(dve.tensor_tensor(norm.half[:, a:b], norm.half[:, a:b], norm.var[:, a:b], ALU.mult))
    chain.link(dve.scalar_tensor_tensor(norm.rstd[:, a:b], norm.half[:, a:b], 1.5, guess, ALU.add, ALU.mult))
    for k, out, sem, before in lanes:
        before()
        dve.tensor_scalar(out, norm.sum[k][:, :], norm.moments[:, k, 0:1], norm.rstd[:, k:k + 1],
                          ALU.subtract, ALU.mult).then_inc(sem, 1)


def pick(ap, t):
    at = slice(t.n, t.n + 1) if isinstance(t.n, int) else bass.ds(t.n, 1)
    return ap[(slice(None), at) + (slice(None),) * (len(ap.shape) - 2)]


def plane(ap, n):
    return ap[n, :, :] if isinstance(n, int) else ap[bass.ds(n, 1), :, :].rearrange("o p n -> p (o n)")


LINKS_A = 12


def turned_count(j, lags=(2, 4, 5)):
    if isinstance(j.n, int):
        return sum(min(max(j.n - lag + 1, 0), j.tiles) for lag in lags)
    return len(lags) * UNROLL * j.q + (len(lags) * (j.m + 1) - sum(lags))


def layer0_attention(nc, io, keep):
    with ExitStack() as ctx:
        new = lambda name, shape, dt=F32: ctx.enter_context(nc.sbuf_tensor(name, shape, dt))
        sems = lambda name: ctx.enter_context(nc.semaphore(name))
        w = lambda name: WEIGHTS.cols(keep.weights, name)
        ps = ctx.enter_context(nc.psum_tensor("ps", [P, 8, 512], F32))

        heads_w = new("heads_w", [P, FIRST.width])
        wqk = new("wqk", [P, AH * D])
        mask = new("mask", [P, TILES, S], I32)
        mask_add = new("mask_add", [P, TILES, S])
        alive = new("alive", [P, TILES])
        bq_scaled = new("bq_scaled", [P, 1])
        before_b = new("before_b", [P, P], BF16)
        ones_b = new("ones_b", [P, P], BF16)
        base = keep.base

        x_nat = [new(f"x_nat{m}", [P, D]) for m in range(UNROLL)]
        x_t = [new(f"x_t{m}", [P, P]) for m in range(UNROLL)]
        ctx_t = [new(f"ctx_t{m}", [P, PER, 2, S]) for m in range(UNROLL)]
        g = new("g", [P, AH, P])
        v = new("v", [P, AH * D])
        sim = new("sim", [P, AH, S])
        x1 = [new(f"x1_{m}", [P, D]) for m in range(2)]
        x1_plus = [new(f"x1_plus{m}", [P, D]) for m in range(UNROLL)]
        q_t = new("q_t", [P, P])
        k_t = new("k_t", [P, P])
        k_heads = new("k_heads", [P, HALF, P])
        e = [new(f"e{m}", [P, XH, S]) for m in range(2)]
        row_max = [new(f"row_max{m}", [P, XH]) for m in range(2)]
        e_t = new("e_t", [P, XH // 2, P])
        v_heads = new("v_heads", [P, PER * 2, HALF // 2 * (VW + 2 * HD)])
        rden = new("rden", [P, 2, HALF])
        mixed = new("mixed", [P, D])
        x2 = [new(f"x2_{m}", [P, D]) for m in range(UNROLL)]
        turned_t = new("turned_t", [P, 3 * P])
        lg = [new(f"lg{m}", [P, E0]) for m in range(UNROLL)]
        top = new("top", [P, 8])
        top_at = new("top_at", [P, 8], U32)
        top_f = new("top_f", [P, 1])
        chosen = new("chosen", [P, E0], BF16)
        rows8 = new("rows8", [P, E0])
        rows8c = new("rows8c", [P, E0])
        row_f = new("row_f", [P, 1])
        row_i = [new(f"row_i{m}", [P, 1], I32) for m in range(UNROLL)]
        norm = Norm(new, sems, "n0", 2)

        weights_loaded, first_loaded = sems("weights_loaded"), sems("first_loaded")
        mask_loaded = sems("mask_loaded")
        fused, wqk_ready, const_ready = sems("fused"), sems("wqk_ready"), sems("const_ready")
        x_loaded = [sems(f"x_loaded{m}") for m in range(UNROLL)]
        x2_stored = [sems(f"x2_stored{m}") for m in range(UNROLL)]
        scattered = [sems(f"scattered{m}") for m in range(UNROLL)]
        (g_done, g_ready, v_done, v_ready, st_done, sim_ready, av_done, attn_added, x1_ready, turned_done, turned_ready,
         q_done, qt_ready, k_done, kt_ready, kexp_ready, v2_done, vexp_ready, s_done, s_read, max_ready, sub_ready,
         e_ready, et_done, et_ready, avx_done, mixed_ready, side_done, x1p_ready,
         xattn_added, x2_ready, lg_read, lg_kept, chosen_ready, rank_done, base_added, row_ready,
         dve_chain) = (sems(n) for n in (
             "g_done", "g_ready", "v_done", "v_ready", "st_done", "sim_ready", "av_done", "attn_added", "x1_ready",
             "turned_done", "turned_ready", "q_done", "qt_ready", "k_done", "kt_ready", "kexp_ready", "v2_done",
             "vexp_ready", "s_done", "s_read", "max_ready", "sub_ready", "e_ready", "et_done", "et_ready",
             "avx_done", "mixed_ready", "side_done", "x1p_ready", "xattn_added",
             "x2_ready", "lg_read", "lg_kept", "chosen_ready", "rank_done", "base_added",
             "row_ready", "dve_chain"))

        g_ps = ps[:, 0:2, :].rearrange("p a n -> p (a n)")
        st_ps = ps[:, 0, :].rearrange("p (h n) -> p h n", h=AH)
        z_ps = ps[:, 0, 0:D]
        v2_ps = ps[:, 1, 0:PER * D]
        v_ps = ps[:, 2:4, :].rearrange("p a n -> p (a n)")
        s_ps = ps[:, 4:6, :]
        mix_ps = ps[:, 4, 0:2 * VW].rearrange("p (g n) -> p g n", g=2)
        turned_ps = ps[:, 6, 0:3 * P]
        q_ps = k_ps = ps[:, 6, 0:P]
        wo_ps = ps[:, 7, 0:D]
        lg_ps = ps[:, 7, P:P + E0]
        rank_ps, total_ps = (ps[:, 7, k * E0:(k + 1) * E0] for k in range(2))

        block = ctx.enter_context(nc.Block())

        @block.sync
        def _(sp):
            sp.dma_start(heads_w[:, :], io.first).then_inc(first_loaded, 16)
            layer0 = WEIGHTS.at["a1_wk_t"][0]
            sp.dma_start(keep.weights[:, 0:layer0], io.weights[:, 0:layer0]).then_inc(weights_loaded, 16)

            def step(j):
                if t := j.tile(0):
                    wait(sp, attn_added, t.n - UNROLL + 1)
                    wait(sp, v2_done, t.n - UNROLL + 1)
                    sp.dma_start(x_t[t.m][:, :], plane(io.x_t, t.n)).then_inc(x_loaded[t.m], 16)
                    sp.dma_start(x_nat[t.m][:, :], plane(io.x, t.n)).then_inc(x_loaded[t.m], 16)
                    sp.dma_start(ctx_t[t.m][:, :, :, :].rearrange("p b c n -> p (b c n)"),
                                 plane(io.ctx_t, t.n)).then_inc(x_loaded[t.m], 16)
                if isinstance(j.n, int) and j.n == 1:
                    sp.dma_start(mask[:, :, :], io.mask).then_inc(mask_loaded, 16)
                if t := j.tile(5):
                    wait(sp, x2_ready, t.n + 1)
                    sp.dma_start(plane(io.x2, t.n), x2[t.m][:, :]).then_inc(x2_stored[t.m], 16)

            run_turns(sp, step, 6, ahead=3)
            for m in range(UNROLL):
                sp.wait_ge(x2_stored[m], 16 * TILES // UNROLL)

        @block.tensor
        def _(pe):
            pe.wait_ge(first_loaded, 16)
            for h in range(AH):
                part = FIRST.cols(heads_w, "wq_heads"), FIRST.cols(heads_w, "wk_heads")
                pe.matmul(g_ps[:, h * D:(h + 1) * D], part[0][:, h * D:(h + 1) * D], part[1][:, h * D:(h + 1) * D],
                          start=True, stop=True).then_inc(fused, 1)
            pe.wait_ge(wqk_ready, 2)
            pe.wait_ge(weights_loaded, 16)
            pe.wait_ge(const_ready, 1)
            ident = w("ident")
            turned = ((2, x1_ready, x1), (4, mixed_ready, [mixed]), (5, x2_ready, x2))

            def step(j):
                if t := j.tile(1):
                    pe.wait_ge(x_loaded[t.m], 48 * (t.q + 1))
                    wait(pe, attn_added, t.n)
                    wait(pe, vexp_ready, 2 * (t.n - 2))
                    for h in range(AH):
                        mm = pe.matmul(g_ps[:, h * P:(h + 1) * P], wqk[:, h * D:(h + 1) * D], x_t[t.m][:, :],
                                       start=True, stop=True)
                        if h % 4 == 3:
                            mm.then_inc(g_done, 1)
                if t := j.tile(1):
                    for b in range(PER):
                        for k in range(2):
                            mm = pe.matmul(v_ps[k * S:(k + 1) * S, b * 512:(b + 1) * 512], x_t[t.m][:, b * S:(b + 1) * S],
                                           w("wv_t")[:, k * 512:(k + 1) * 512], start=True, stop=True)
                        mm.then_inc(v_done, 1)
                wait(pe, kt_ready, j.n - 1 if not isinstance(j.n, int) else min(j.n - 1, TILES))
                for k, (lag, ready, src) in enumerate(turned):
                    if t := j.tile(lag):
                        pe.wait_ge(ready, t.n + 1)
                        pe.transpose(turned_ps[:, k * P:(k + 1) * P], src[t.m % len(src)][:, :],
                                     ident).then_inc(turned_done, 1)
                if t := j.tile(1):
                    pe.wait_ge(g_ready, 2 * t.n + 2)
                    for b in range(PER):
                        for k in range(2):
                            mm = pe.matmul(st_ps[k * S:(k + 1) * S, 4 * b:4 * b + 4, :], x_t[t.m][:, b * S:(b + 1) * S],
                                           g[:, 4 * k:4 * k + 4, b * S:(b + 1) * S], start=True, stop=True)
                    mm.then_inc(st_done, 1)
                if t := j.tile(2):
                    pe.wait_ge(turned_ready, t.n + 1)
                    pe.matmul(q_ps, w("x0_wq"), turned_t[:, 0:P], start=True, stop=True).then_inc(q_done, 1)
                if t := j.tile(3):
                    for b in range(PER):
                        mm = pe.matmul(v2_ps[:, b * D:(b + 1) * D], ctx_t[t.m][:, b, :, :].rearrange("p c n -> p (c n)"),
                                       w("x0_wv"), start=True, stop=True)
                    mm.then_inc(v2_done, 1)
                if t := j.tile(4):
                    pe.wait_ge(turned_ready, t.n + 3)
                    wait(pe, base_added, t.n - 1)
                    wait(pe, xattn_added, t.n)
                    mm = pe.matmul(wo_ps, turned_t[:, P:2 * P], w("x0_wo"), start=True, stop=True)
                if t := j.tile(5):
                    pe.wait_ge(turned_ready, t.n + 4)
                    wait(pe, base_added, t.n)
                    wait(pe, xattn_added, t.n + 1)
                    mm = pe.matmul(lg_ps, turned_t[:, 2 * P:3 * P], w("gate_w"), start=True, stop=True)
                if j.tile(4) or j.tile(5):
                    mm.then_inc(side_done, 1)
                if t := j.tile(2):
                    pe.wait_ge(qt_ready, t.n + 1)
                    pe.wait_ge(kexp_ready, t.n + 1)
                    wait(pe, s_read, t.n)
                    wait(pe, mixed_ready, t.n - 1)
                if t := j.tile(1):
                    wait(pe, kt_ready, t.n)
                    pe.matmul(k_ps, w("x0_wk"), ctx_t[t.m][:, :, 0, :], start=True, stop=True).then_inc(k_done, 1)
                if t := j.tile(2):
                    for r in range(2):
                        for b in range(PER):
                            mm = pe.matmul(s_ps[b * S:(b + 1) * S, r, :], q_t[r * S:(r + 1) * S, b * S:(b + 1) * S],
                                           k_heads[r * S:(r + 1) * S, :, b * S:(b + 1) * S], start=True, stop=True)
                    mm.then_inc(s_done, 1)
                if t := j.tile(3):
                    pe.wait_ge(e_ready, t.n + 1)
                    wait(pe, v_ready, 2 * (t.n + 3) if not isinstance(t.n, int) else 2 * min(t.n + 3, TILES))
                    e_flat = e[t.m % 2][:, :, :].rearrange("p h n -> p (h n)")
                    for c in range(XH // 2):
                        mm = pe.transpose(v_ps[:, c * P:(c + 1) * P], e_flat[:, c * P:(c + 1) * P], ident)
                        if c % 4 == 3:
                            mm.then_inc(et_done, 1)
                if t := j.tile(1):
                    pe.wait_ge(sim_ready, t.n + 1)
                    pe.wait_ge(v_ready, 2 * t.n + 2)
                    for c in range(AH // 2):
                        for b in range(PER):
                            mm = pe.matmul(z_ps[b * S:(b + 1) * S, :], sim[:, 4 * b + c, :],
                                           v[:, b * 512 + c * D:b * 512 + (c + 1) * D], start=(c == 0), stop=(c == AH // 2 - 1))
                    mm.then_inc(av_done, 1)
                if t := j.tile(3):
                    pe.wait_ge(vexp_ready, 2 * t.n + 2)
                    wait(pe, s_read, t.n + 2 if not isinstance(t.n, int) else min(t.n + 2, TILES))
                    for c in range(XH // 2):
                        if c % 4 == 0:
                            pe.wait_ge(et_ready, 2 * t.n + c // 4 + 1)
                        for b in range(PER):
                            mm = pe.matmul(mix_ps[b * S:(b + 1) * S, c // 4, :], e_t[:, c, b * S:(b + 1) * S],
                                           v_heads[:, 2 * b + c // 4, c % 4 * VW:(c % 4 + 1) * VW],
                                           start=(c % 4 == 0), stop=(c % 4 == 3))
                    mm.then_inc(avx_done, 1)
                if t := j.tile(5):
                    pe.wait_ge(chosen_ready, t.n + 1)
                    wait(pe, lg_read, t.n + 1)
                    wait(pe, xattn_added, t.n + 2 if not isinstance(t.n, int) else min(t.n + 2, TILES))
                    pe.matmul(rank_ps, before_b[:, :], chosen[:, :], start=True, stop=True)
                    pe.matmul(total_ps, ones_b[:, :], chosen[:, :], start=True, stop=True).then_inc(rank_done, 1)

            run_turns(pe, step, 6, ahead=3)

        @block.scalar
        def _(act):
            act.preload_act_table_set("natural_log_exp_and_others")
            layer0 = WEIGHTS.at["a1_wk_t"][0]
            later = [(keep.w1[:, :, :], io.w1), (keep.w2[:, :, :, :], io.w2), (keep.b1[:, :, :], io.b1),
                     (keep.b2[:, :, :], io.b2), (keep.weights[:, layer0:], io.weights[:, layer0:])]
            for c in range(2):
                act.wait_ge(fused, 4 * c + 4)
                act.activation(wqk[:, c * 512:(c + 1) * 512], g_ps[:, c * 512:(c + 1) * 512],
                               ACT.Copy).then_inc(wqk_ready, 1)
            act.wait_ge(const_ready, 1)

            def keep_v(t, c):
                act.wait_ge(v_done, 2 * t.n + c + 1)
                act.activation(v[:, c * 512:(c + 1) * 512], v_ps[:, c * 512:(c + 1) * 512], ACT.Copy).then_inc(v_ready, 1)

            def step(j):
                if isinstance(j.n, int) and j.n > 2 and later:
                    to, source = later.pop(0)
                    act.dma_start(to, source).then_inc(keep.ffn_loaded, 16)
                if t := j.tile(1):
                    for c in range(2):
                        act.wait_ge(g_done, 2 * t.n + c + 1)
                        act.activation(g[:, 4 * c:4 * c + 4, :].rearrange("p h n -> p (h n)"),
                                       g_ps[:, c * 512:(c + 1) * 512], ACT.Copy).then_inc(g_ready, 1)
                if t := j.tile(3):
                    act.wait_ge(sub_ready, t.n + 1)
                    act.activation(e[t.m % 2][:, :, :], e[t.m % 2][:, :, :], ACT.Exp).then_inc(e_ready, 1)
                if t := j.tile(1):
                    keep_v(t, 0)
                here = [k for k, lag in enumerate((2, 4, 5)) if j.tile(lag)]
                if here:
                    act.wait_ge(turned_done, turned_count(j))
                    r = slice(here[0] * P, (here[-1] + 1) * P)
                    act.activation(turned_t[:, r], turned_ps[:, r], ACT.Copy).then_inc(turned_ready, 1)
                if t := j.tile(1):
                    keep_v(t, 1)
                if t := j.tile(2):
                    act.wait_ge(q_done, t.n + 1)
                    act.activation(q_t[:, :], q_ps, ACT.Identity, bias=bq_scaled[:, 0:1],
                                   scale=HD ** -0.5).then_inc(qt_ready, 1)
                if t := j.tile(1):
                    act.wait_ge(k_done, t.n + 1)
                    wait(act, kexp_ready, t.n)
                    act.activation(k_t[:, :], k_ps, ACT.Identity, bias=w("x0_bk")).then_inc(kt_ready, 1)
                if t := j.tile(3):
                    act.wait_ge(et_done, 2 * t.n + 1)
                    act.activation(e_t[:, 0:4, :].rearrange("p h n -> p (h n)"), v_ps[:, 0:512],
                                   ACT.Copy).then_inc(et_ready, 1)
                if t := j.tile(3):
                    act.wait_ge(et_done, 2 * t.n + 2)
                    act.activation(e_t[:, 4:8, :].rearrange("p h n -> p (h n)"), v_ps[:, 512:1024],
                                   ACT.Copy).then_inc(et_ready, 1)
                if j.tile(1) or j.tile(4):
                    norm_scalar(act, norm, j.n, 0 if j.tile(1) else 1, 2 if j.tile(4) else 1)

            run_turns(act, step, 6, ahead=3)

        @block.gpsimd
        def _(pool):
            pool.wait_ge(weights_loaded, 16)

            def step(j):
                if t := j.tile(2):
                    pool.wait_ge(kt_ready, t.n + 1)
                    wait(pool, s_done, t.n)
                    pool.tensor_tensor(k_heads[:, :, :], spread(k_t[:, :], 1, HALF),
                                       spread(w("head_of_row"), 2, P), ALU.mult).then_inc(kexp_ready, 1)
                if t := j.tile(6):
                    pool.wait_ge(row_ready, t.n + 1)
                if t := j.tile(2):
                    pool.wait_ge(x1_ready, t.n + 1)
                    wait(pool, xattn_added, t.n - UNROLL + 1)
                    pool.tensor_tensor(x1_plus[t.m][:, :], x1[t.m % 2][:, :], w("x0_bo"), ALU.add).then_inc(x1p_ready, 1)
                if t := j.tile(6):
                    pool.indirect_dma_start(io.sorted, bass.IndirectOffsetOnAxis(ap=row_i[t.m][:, 0:1], axis=0),
                                            x2[t.m][:, :], None).then_inc(scattered[t.m], 16)
                if t := j.tile(5):
                    pool.wait_ge(lg_read, t.n + 1)
                    pool.tensor_copy(pick(keep.logits, t).rearrange("p o n -> p (o n)"), lg[t.m][:, :]).then_inc(lg_kept, 1)
                if t := j.tile(2):
                    pool.wait_ge(max_ready, t.n + 1)
                    pool.tensor_tensor(e[t.m % 2][:, :, :], e[t.m % 2][:, :, :], spread(row_max[t.m % 2][:, :], 2, S),
                                       ALU.subtract).then_inc(sub_ready, 1)

            run_turns(pool, step, 6, ahead=3)
            for m in range(UNROLL):
                pool.wait_ge(scattered[m], 16 * TILES // UNROLL)

        @block.vector
        def _(dve):
            chain = Chain(dve, dve_chain)
            dve.memset(norm.idle[:, :], 0.0)
            dve.memset(v_heads[:, :, :], 0.0)
            dve.memset(ones_b[:, :], 1.0)
            dve.wait_ge(weights_loaded, 16)
            dve.tensor_copy(before_b[:, :], w("before"))
            dve.tensor_copy(base[:, :], w("region"))
            zeroed = chain.mark(dve.tensor_scalar(bq_scaled[:, :], w("x0_bq"), HD ** -0.5, None, ALU.mult))
            chain.wait(zeroed)
            for half in range(PER * 2):
                pairs = v_heads[:, half, 0:HALF // 2 * VW].rearrange("p (c n) -> p c n", n=VW)
                last = dve.tensor_copy(pairs[:, :, HALF * HD:VW], w("ones_at").rearrange("p (c n) -> p c n", n=HALF))
            last.then_inc(const_ready, 1)
            def value_half(r):
                rows = slice(r * S, (r + 1) * S)
                pairs = "p (g c h n) -> p g c h n"
                src = v2_ps[rows, :].rearrange(pairs, g=2 * PER, c=HALF // 2, h=2)[:, :, :, r, :]
                bias = w("x0_bv")[rows, :].rearrange(pairs, g=2 * PER, c=HALF // 2, h=2)[:, :, :, r, :]
                own = v_heads[rows, :, :].rearrange("p g (c n) -> p g c n", c=HALF // 2)[:, :, :, r * HD:(r + 1) * HD]
                dve.tensor_tensor(own, src, bias, ALU.add).then_inc(vexp_ready, 1)

            def step(j):
                if t := j.tile(6):
                    dve.wait_ge(rank_done, t.n + 1)
                    rows_sum = chain.mark(dve.tensor_tensor(rows8[:, :], rank_ps, base[:, :], ALU.add))
                    dve.tensor_tensor(base[:, :], base[:, :], total_ps, ALU.add).then_inc(base_added, 1)
                    chain.wait(rows_sum)
                    row = chain.mark(dve.tensor_tensor_reduce(out=rows8c[:, :], in0=rows8[:, :], in1=chosen[:, :],
                                                              scale=1.0, scalar=0.0, op0=ALU.mult, op1=ALU.add,
                                                              accum_out=row_f[:, 0:1]))

                if t := j.tile(1):
                    dve.wait_ge(st_done, t.n + 1)
                    dve.scalar_tensor_tensor(sim[:, :, :], st_ps, 0.0, spread(w("causal"), 1, AH), ALU.max,
                                             ALU.mult).then_inc(sim_ready, 1)
                if t := j.tile(6):
                    chain.wait(row)
                    wait(dve, scattered[t.m], 16 * t.q)
                    dve.tensor_copy(row_i[t.m][:, :], row_f[:, :]).then_inc(row_ready, 1)
                    dve.tensor_copy(pick(keep.rows[:, :], t), row_f[:, :])
                if t := j.tile(5):
                    dve.wait_ge(side_done, t.n + 2)
                    wait(dve, lg_kept, t.n - 1)
                    dve.tensor_tensor(lg[t.m][:, :], lg_ps, w("gate_b"), ALU.add).then_inc(lg_read, 1)
                    dve.wait_ge(lg_read, t.n + 1)
                if t := j.tile(3):
                    dve.wait_ge(v2_done, t.n + 1)
                    wait(dve, avx_done, t.n)
                    value_half(0)
                    value_half(1)
                if t := j.tile(5):
                    topped = chain.mark(dve.max(out=top[:, :], in_=lg[t.m][:, :]))
                if j.tile(5):
                    chain.wait(topped)
                if isinstance(j.n, int) and j.n == 2:
                    dve.wait_ge(mask_loaded, 16)
                    chain.link(dve.tensor_scalar(mask_add[:, :, :], mask[:, :, :], 0, -1e20, ALU.is_equal, ALU.mult))
                    chain.link(dve.tensor_reduce(alive[:, :], mask_add[:, :, :], axis=AX.X, op=ALU.max))
                    chain.link(dve.tensor_scalar(alive[:, :], alive[:, :], 0.0, None, ALU.is_equal))
                    chain.link(dve.tensor_tensor(mask_add[:, :, :], mask_add[:, :, :], spread(alive[:, :], 2, S), ALU.mult))
                if t := j.tile(2):
                    dve.wait_ge(s_done, t.n + 1)
                    wait(dve, et_done, 2 * (t.n - 1))
                    dve.scalar_tensor_tensor(e[t.m % 2][:, :, :], s_ps[:, :, :].rearrange("p r (h n) -> p (r h) n", h=HALF),
                                             pick(alive, t), pick(mask_add, t).broadcast_to([P, XH, S]),
                                             ALU.mult, ALU.add).then_inc(s_read, 1)
                if t := j.tile(5):
                    found = chain.mark(dve.max_index(out=top_at[:, :], in_max=top[:, :], in_values=lg[t.m][:, :]))
                if t := j.tile(5):
                    chain.wait(found)
                    chain.link(dve.tensor_copy(top_f[:, :], top_at[:, 0:1]))
                    wait(dve, rank_done, t.n)
                    dve.tensor_scalar(chosen[:, :], w("expert_no"), top_f[:, 0:1], None,
                                      ALU.is_equal).then_inc(chosen_ready, 1)
                lanes = []
                if t := j.tile(4):
                    dve.wait_ge(side_done, t.n + 1)
                    dve.wait_ge(x1p_ready, t.n + 1)
                    dve.tensor_tensor(norm.sum[1][:, :], wo_ps, x1_plus[t.m][:, :], ALU.add).then_inc(xattn_added, 1)
                    def free2(t=t):
                        wait(dve, x2_stored[t.m], 16 * t.q)
                        wait(dve, scattered[t.m], 16 * t.q)
                    lanes.append((1, x2[t.m][:, :], x2_ready, free2))
                if t := j.tile(1):
                    dve.wait_ge(av_done, t.n + 1)
                    dve.scalar_tensor_tensor(norm.sum[0][:, :], x_nat[t.m][:, :], 2.0, z_ps, ALU.mult,
                                             ALU.add).then_inc(attn_added, 1)
                    def free1(t=t):
                        wait(dve, x1p_ready, t.n - 1)
                    lanes.append((0, x1[t.m % 2][:, :], x1_ready, free1))
                if t := j.tile(2):
                    dve.wait_ge(s_read, t.n + 1)
                    wait(dve, sub_ready, t.n - 1)
                    dve.tensor_reduce(row_max[t.m % 2][:, :], e[t.m % 2][:, :, :], axis=AX.X, op=ALU.max).then_inc(max_ready, 1)
                if lanes:
                    lanes.sort(key=lambda lane: lane[0])
                    if t := j.tile(4):
                        dve.wait_ge(xattn_added, t.n + 1)
                    if t := j.tile(1):
                        dve.wait_ge(attn_added, t.n + 1)
                    norm_vector(dve, chain, norm, j.n, lanes)
                if t := j.tile(3):
                    dve.wait_ge(avx_done, t.n + 1)
                    chain.link(dve.reciprocal(rden[:, :, :], mix_ps[:, :, HALF * HD:VW]))
                    dve.tensor_tensor(mixed[:, :].rearrange("p (g h n) -> p g h n", g=2, h=HALF),
                                      mix_ps[:, :, 0:HALF * HD].rearrange("p g (h n) -> p g h n", h=HALF),
                                      spread(rden[:, :, :], 3, HD), ALU.mult).then_inc(mixed_ready, 1)

            run_turns(dve, step, 6, chain, LINKS_A, ahead=3)


LINKS_B = 0


def layer0_experts(nc, io, keep):
    with ExitStack() as ctx:
        new = lambda name, shape, dt=F32: ctx.enter_context(nc.sbuf_tensor(name, shape, dt))
        sems = lambda name: ctx.enter_context(nc.semaphore(name))
        w = lambda name: WEIGHTS.cols(keep.weights, name)
        ps = ctx.enter_context(nc.psum_tensor("ps_b", [P, 8, 512], F32))
        idle = SLOTS - ROWS // P
        dummy = E0 * REGION

        count = new("count", [P, E0])
        fills = new("fills", [P, E0, TILES])
        slots = new("slots", [P, E0])
        less = new("less", [P, E0])
        rows_f = new("rows_f", [P, TILES])
        behind = new("behind", [P, TILES, E0])
        skipped = new("skipped", [P, TILES])
        ends = [new(f"ends{k}", [1, E0]) for k in range(1, 4)]
        first_row = new("first_row", [1, E0])
        past = new("past", [1, SLOTS, E0])
        expert_f = new("expert_f", [1, SLOTS])
        unused = new("unused", [1, SLOTS])
        row_f = new("row_f_b", [1, SLOTS])
        expert_i = new("expert_i", [1, SLOTS], I32)
        row_i = new("row_i_b", [1, SLOTS], I32)
        pad_i = new("pad_i", [1, E0], I32)
        zeros = new("zeros", [P, D])
        best = new("best", [P, TILES])
        shifted = new("shifted", [P, TILES, E0])
        total = new("total", [P, TILES])

        xs = [new(f"xs{m}", [P, D]) for m in range(UNROLL)]
        xs_t = [new(f"xs_t{m}", [P, P]) for m in range(2)]
        h = [new(f"h{m}", [P, M0]) for m in range(2)]
        h_t = [new(f"h_t{m}", [P, CH, P]) for m in range(2)]
        y = [new(f"y{m}", [P, D]) for m in range(UNROLL)]

        loaded = [sems(f"xs_loaded{m}") for m in range(UNROLL)]
        stored = [sems(f"y_stored{m}") for m in range(UNROLL)]
        (pads_ready, tables_ready, pads_zeroed, xt_done, xt_ready, h_done, h_ready, ht_done, ht_ready, y_done, y_ready,
         best_ready, exp_ready, chain_b) = (sems(n) for n in (
             "pads_ready", "tables_ready", "pads_zeroed", "xt_done", "xt_ready", "h_done", "h_ready", "ht_done",
             "ht_ready", "y_done", "y_ready", "best_ready", "exp_ready", "chain_b"))

        block = ctx.enter_context(nc.Block())

        def number(eng, table, t, most):
            at = slice(t.n, t.n + 1) if isinstance(t.n, int) else bass.ds(t.n, 1)
            return eng.value_load(table[0:1, at], min_val=0, max_val=most)

        def zero_pads(eng, experts):
            for k in experts:
                row = eng.value_load(pad_i[0:1, k:k + 1], min_val=0, max_val=dummy)
                eng.dma_start(io.sorted[bass.ds(row, P), :], zeros[:, :]).then_inc(pads_zeroed, 16)

        @block.sync
        def _(sp):
            sp.wait_ge(pads_ready, 1)
            zero_pads(sp, range(0, E0, 2))
            sp.wait_ge(pads_zeroed, 16 * E0)
            sp.wait_ge(tables_ready, 1)

            def step(j):
                if isinstance(j.n, int) and j.n == UNROLL:
                    for k in range(idle):
                        sp.dma_start(io.sorted[dummy + k * P:dummy + (k + 1) * P, :], zeros[:, :]).then_inc(pads_zeroed, 16)
                if isinstance(j.n, int) and j.n == 2 * UNROLL:
                    sp.wait_ge(pads_zeroed, 16 * (E0 + idle))
                if t := j.tile(0):
                    wait(sp, xt_done, t.n - UNROLL + 1)
                    row = number(sp, row_i, t, dummy + (idle - 1) * P)
                    sp.dma_start(xs[t.m][:, :], io.sorted[bass.ds(row, P), :]).then_inc(loaded[t.m], 16)
                if t := j.tile(5):
                    sp.wait_ge(y_ready, t.n + 1)
                    sp.dma_start(plane(io.y.rearrange("(t p) d -> t p d", p=P), t.n), y[t.m][:, :]).then_inc(stored[t.m], 16)

            run_turns(sp, step, 5, tiles=SLOTS, ahead=4)
            for m in range(UNROLL):
                sp.wait_ge(stored[m], 16 * SLOTS // UNROLL)
            sp.wait_ge(keep.ffn_loaded, 80)

        @block.tensor
        def _(pe):
            pe.wait_ge(keep.ffn_loaded, 80)
            pe.wait_ge(tables_ready, 1)

            ahead = {}

            def step(j):
                if t := j.tile(3):
                    expert = ahead.pop("expert") if ahead else number(pe, expert_i, t, E0 - 1)
                    pe.wait_ge(xt_ready, t.n + 1)
                    wait(pe, h_ready, t.n - 1)
                    pe.matmul(ps[:, 2 + t.m % 2, :], xs_t[t.m % 2][:, :],
                              keep.w1[:, bass.ds(expert, 1), :].rearrange("p o n -> p (o n)"),
                              start=True, stop=True).then_inc(h_done, 1)
                if t := j.tile(5):
                    expert = number(pe, expert_i, t, E0 - 1)
                if t := j.tile(2):
                    pe.wait_ge(loaded[t.m], 16 * (t.q + 1))
                    wait(pe, xt_ready, t.n - 1)
                    pe.transpose(ps[:, t.m % 2, 0:P], xs[t.m][:, :], w("ident")).then_inc(xt_done, 1)
                if t := j.tile(4):
                    pe.wait_ge(h_ready, t.n + 1)
                    wait(pe, ht_ready, t.n - 1)
                    for c in range(CH):
                        mm = pe.transpose(ps[:, 4 + t.m % 2, c * P:(c + 1) * P], h[t.m % 2][:, c * P:(c + 1) * P], w("ident"))
                    mm.then_inc(ht_done, 1)
                if j.m < UNROLL - 1 and (t := Turn(j.q, j.m + 1, SLOTS).tile(3)):
                    ahead["expert"] = number(pe, expert_i, t, E0 - 1)
                if t := j.tile(5):
                    pe.wait_ge(ht_ready, t.n + 1)
                    wait(pe, y_ready, t.n - 1)
                    for c in range(CH):
                        mm = pe.matmul(ps[:, 6 + t.m % 2, 0:D], h_t[t.m % 2][:, c, :],
                                       keep.w2[:, bass.ds(expert, 1), c, :].rearrange("p o n -> p (o n)"),
                                       start=(c == 0), stop=(c == CH - 1))
                    mm.then_inc(y_done, 1)

            run_turns(pe, step, 5, tiles=SLOTS, ahead=4)

        @block.scalar
        def _(act):
            act.wait_ge(pads_ready, 1)
            zero_pads(act, range(1, E0, 2))
            act.wait_ge(best_ready, 1)
            act.activation(shifted[:, :, :], shifted[:, :, :], ACT.Exp).then_inc(exp_ready, 1)

            def step(j):
                if t := j.tile(2):
                    act.wait_ge(xt_done, t.n + 1)
                    wait(act, h_done, t.n - 1)
                    act.activation(xs_t[t.m % 2][:, :], ps[:, t.m % 2, 0:P], ACT.Copy).then_inc(xt_ready, 1)
                if t := j.tile(4):
                    act.wait_ge(ht_done, t.n + 1)
                    wait(act, y_done, t.n - 1)
                    act.activation(h_t[t.m % 2][:, :, :].rearrange("p c n -> p (c n)"), ps[:, 4 + t.m % 2, :],
                                   ACT.Relu).then_inc(ht_ready, 1)

            run_turns(act, step, 5, tiles=SLOTS, ahead=4)

        @block.vector
        def _(dve):
            chain = Chain(dve, chain_b)
            link = chain.link
            dve.memset(zeros[:, :], 0.0)
            dve.tensor_copy(pad_i[:, :], keep.base[0:1, :]).then_inc(pads_ready, 1)
            link(dve.tensor_tensor(count[:, :], keep.base[:, :], w("region"), ALU.subtract))
            link(dve.tensor_tensor(fills[:, :, :], spread(count[:, :], 2, TILES), spread(w("tile_rows"), 1, E0), ALU.is_gt))
            link(dve.tensor_reduce(slots[:, :], fills[:, :, :], axis=AX.X, op=ALU.add))
            for k in range(3):
                a, b, by = ends[k - 1] if k else slots[0:1, :], ends[k], 1 << k
                dve.tensor_copy(b[:, 0:by], a[:, 0:by])
                link(dve.tensor_tensor(b[:, by:E0], a[:, by:E0], a[:, 0:E0 - by], ALU.add))
            link(dve.tensor_tensor(past[:, :, :], spread(w("slot_no")[0:1, :], 2, E0), spread(ends[2][:, :], 1, SLOTS), ALU.is_ge))
            link(dve.tensor_reduce(expert_f[:, :], past[:, :, :], axis=AX.X, op=ALU.add))
            link(dve.tensor_tensor(first_row[:, :], slots[0:1, :], ends[2][:, :], ALU.subtract))
            link(dve.scalar_tensor_tensor(first_row[:, :], first_row[:, :], float(P), w("region")[0:1, :], ALU.mult, ALU.add))
            link(dve.tensor_tensor(past[:, :, :], spread(expert_f[:, :], 2, E0), spread(w("expert_no")[0:1, :], 1, SLOTS), ALU.is_equal))
            link(dve.tensor_tensor(past[:, :, :], past[:, :, :], spread(first_row[:, :], 1, SLOTS), ALU.mult))
            link(dve.tensor_reduce(row_f[:, :], past[:, :, :], axis=AX.X, op=ALU.add))
            link(dve.scalar_tensor_tensor(row_f[:, :], w("slot_no")[0:1, :], float(P), row_f[:, :], ALU.mult, ALU.add))
            link(dve.tensor_scalar(unused[:, :], expert_f[:, :], float(E0), float(dummy - ROWS), ALU.is_ge, ALU.mult))
            dve.tensor_tensor(row_i[:, :], row_f[:, :], unused[:, :], ALU.add)
            dve.tensor_scalar(expert_i[:, :], expert_f[:, :], float(E0 - 1), None, ALU.min)
            link(dve.tensor_scalar(unused[:, :], unused[:, :], 1.0, None, ALU.mult))
            dve.tensor_scalar(count[:, :], count[:, :], 1.0, None, ALU.mult).then_inc(tables_ready, 1)
            dve.tensor_scalar(less[:, :], slots[:, :], -float(P), float(REGION), ALU.mult, ALU.add)
            link(dve.tensor_copy(rows_f[:, :], keep.rows[:, :]))
            link(dve.tensor_tensor(behind[:, :, 1:E0], spread(rows_f[:, :], 2, E0 - 1), spread(w("region")[:, 1:E0], 1, TILES), ALU.is_ge))
            link(dve.tensor_tensor(behind[:, :, 1:E0], behind[:, :, 1:E0], spread(less[:, 0:E0 - 1], 1, TILES), ALU.mult))
            link(dve.tensor_reduce(skipped[:, :], behind[:, :, 1:E0], axis=AX.X, op=ALU.add))
            dve.tensor_tensor(keep.rows[:, :], rows_f[:, :], skipped[:, :], ALU.subtract)
            link(dve.tensor_reduce(best[:, :], keep.logits[:, :, :], axis=AX.X, op=ALU.max))
            dve.tensor_tensor(shifted[:, :, :], keep.logits[:, :, :], spread(best[:, :], 2, E0),
                              ALU.subtract).then_inc(best_ready, 1)
            dve.wait_ge(exp_ready, 1)
            link(dve.tensor_reduce(total[:, :], shifted[:, :, :], axis=AX.X, op=ALU.add))
            dve.reciprocal(keep.prob[:, :], total[:, :])

            def step(j):
                if t := j.tile(3):
                    expert = number(dve, expert_i, t, E0 - 1)
                    dve.wait_ge(h_done, t.n + 1)
                    wait(dve, ht_done, t.n - 1)
                    dve.tensor_tensor(h[t.m % 2][:, :], ps[:, 2 + t.m % 2, :],
                                      keep.b1[:, bass.ds(expert, 1), :].rearrange("p o n -> p (o n)"), ALU.add).then_inc(h_ready, 1)
                if t := j.tile(5):
                    expert = number(dve, expert_i, t, E0 - 1)
                    dve.wait_ge(y_done, t.n + 1)
                    wait(dve, stored[t.m], 16 * t.q)
                    dve.tensor_tensor(y[t.m][:, :], ps[:, 6 + t.m % 2, 0:D],
                                      keep.b2[:, bass.ds(expert, 1), :].rearrange("p o n -> p (o n)"), ALU.add).then_inc(y_ready, 1)

            run_turns(dve, step, 5, tiles=SLOTS, ahead=4)


LINKS_C = 10
C_LAGS = (2, 3, 8)


def layer1(nc, io, keep):
    with ExitStack() as ctx:
        new = lambda name, shape, dt=F32: ctx.enter_context(nc.sbuf_tensor(name, shape, dt))
        sems = lambda name: ctx.enter_context(nc.semaphore(name))
        w = lambda name: WEIGHTS.cols(keep.weights, name)
        ps = ctx.enter_context(nc.psum_tensor("ps_c", [P, 8, 512], F32))

        wvo = new("wvo", [P, D])
        bvo = new("bvo", [P, D])
        bv_wide = new("bv_wide", [P, P])
        head_scaled = new("head_scaled", [P, HALF])
        idx = [new(f"idx{m}", [P, 1], I32) for m in range(2)]
        y = [new(f"y_in{m}", [P, D]) for m in range(2)]
        x2 = [new(f"x2_in{m}", [P, D]) for m in range(2)]
        ctx_t = [new(f"ctx_c{m}", [P, P]) for m in range(UNROLL)]
        x3 = [new(f"x3_{m}", [P, D]) for m in range(2)]
        x3_plus = [new(f"x3_plus{m}", [P, D]) for m in range(2)]
        x4 = [new(f"x4_{m}", [P, D]) for m in range(UNROLL)]
        x4_plus = [new(f"x4_plus{m}", [P, D]) for m in range(UNROLL)]
        x5 = [new(f"x5_{m}", [P, D]) for m in range(2)]
        result = [new(f"result{m}", [P, D]) for m in range(2)]
        turned_t = new("turned_c", [P, 3 * P])
        k_t, q_t = new("k_tc", [P, P]), new("q_tc", [P, P])
        v = new("v_c", [P, D])
        sim = new("sim_c", [P, P])
        xk_t = new("xk_t", [P, 2, P])
        xk = [new(f"xk{m}", [P, D]) for m in range(2)]
        xq_t = new("xq_t", [P, 2, S])
        q_heads = new("q_heads", [P, 2, HALF, S])
        e = [new(f"e_c{m}", [P, XH, S]) for m in range(UNROLL)]
        row_max = [new(f"row_max_c{m}", [P, XH]) for m in range(2)]
        rden = new("rden_c", [P, XH])
        rsum = new("rsum_c", [P, XH])
        v_heads = new("v_heads_c", [P, 2, HALF * (HALF * HD + HD)])
        mix_t = new("mix_t", [P, P])
        hid = new("hid", [M1, P])
        hid2 = new("hid2", [M1, P])
        top = [new(f"top_c{m}", [P, 8]) for m in range(UNROLL)]
        norm = Norm(new, sems, "n1", 4)

        x_loaded = [sems(f"xc_loaded{m}") for m in range(2)]
        gathered = [sems(f"gathered{m}") for m in range(2)]
        ctx_loaded = [sems(f"ctx_loaded{m}") for m in range(UNROLL)]
        out_stored = [sems(f"out_stored{m}") for m in range(2)]
        x5_stored = [sems(f"x5_stored{m}") for m in range(2)]
        names = ("idx_ready fused const_ready x3_added x3_ready x3p_ready turned_done turned_ready kq_done kq_ready "
                 "xq_ready side_done xkt_done xkt_ready hid_relu hid_ready rows_done v_ready xk_ready top_ready gap_ready st_done "
                 "sim_ready sums_done attn_added x4_ready x4p_ready qexp_ready s_done s_read max_ready sub_ready "
                 "e_ready vexp_ready mix_done mix_ready xattn_added x5_ready ffn_added out_ready chain").split()
        (idx_ready, fused, const_ready, x3_added, x3_ready, x3p_ready, turned_done, turned_ready, kq_done, kq_ready,
         xq_ready, side_done, xkt_done, xkt_ready, hid_relu, hid_ready, rows_done, v_ready, xk_ready, top_ready, gap_ready, st_done,
         sim_ready, sums_done, attn_added, x4_ready, x4p_ready, qexp_ready, s_done, s_read, max_ready, sub_ready,
         e_ready, vexp_ready, mix_done, mix_ready, xattn_added, x5_ready, ffn_added, out_ready,
         chain_c) = (sems(n + "_c") for n in names)

        k_ps, q_ps = (ps[:, 0, k * P:(k + 1) * P] for k in range(2))
        xq_ps = ps[:, 6, 2 * P:3 * P]
        xq_ps = xq_ps.rearrange("p (r n) -> p r n", r=2)
        v_ps, xk_ps, lg_ps = ps[:, 1, 0:D], ps[:, 1, D:2 * D], ps[:, 1, 2 * D:2 * D + E1]
        st_ps = z_ps = ps[:, 2, 0:P]
        ffn_ps, wo_ps = ps[:, 2, P:2 * P], ps[:, 2, 2 * P:3 * P]
        xkt_ps, hid_ps = ps[:, 7, P:2 * P].rearrange("p (r n) -> p r n", r=2), ps[0:M1, 6, P:2 * P]
        s_ps = ps[:, 4:6, :]
        turned_ps = ps[:, 7, 2 * P:3 * P], ps[:, 3, 0:P], ps[:, 3, P:2 * P]
        mix_ps = ps[:, 3, 2 * P:2 * P + S], ps[:, 7, 0:S]

        block = ctx.enter_context(nc.Block())
        LAGS = 8

        def before(j, lag):
            if isinstance(j.n, int):
                return min(max(j.n - lag, 0), TILES)
            return UNROLL * j.q + (j.m - lag)

        def turns(j, lag):
            return max(j.n - lag + 1, 0) if isinstance(j.n, int) else UNROLL * j.q + (j.m - lag + 1)

        def turned_before(j, ahead=0):
            if isinstance(j.n, int):
                return min(max(j.n + ahead - 2, 0), TILES) + max(j.n + ahead - 3, 0)
            return 2 * UNROLL * j.q + (2 * (j.m + ahead) - 5)

        @block.sync
        def _(sp):
            def step(j):
                if t := j.tile(0):
                    wait(sp, x3_added, t.n - 1)
                    sp.dma_start(x2[t.m % 2][:, :], plane(io.x2, t.n)).then_inc(x_loaded[t.m % 2], 16)
                if t := j.tile(2):
                    wait(sp, xk_ready, t.n - UNROLL + 1)
                    sp.dma_start(ctx_t[t.m][:, :], plane(io.ctx_p, t.n)).then_inc(ctx_loaded[t.m], 16)
                if t := j.tile(8):
                    sp.wait_ge(x5_ready, t.n + 1)
                    sp.dma_start(plane(io.x5, t.n), x5[t.m % 2][:, :]).then_inc(x5_stored[t.m % 2], 16)
                    sp.wait_ge(out_ready, t.n + 1)
                    sp.dma_start(plane(io.out, t.n), result[t.m % 2][:, :]).then_inc(out_stored[t.m % 2], 16)

            run_turns(sp, step, LAGS, ahead=2)
            for m in range(2):
                sp.wait_ge(out_stored[m], 16 * TILES // 2)
                sp.wait_ge(x5_stored[m], 16 * TILES // 2)

        @block.tensor
        def _(pe):
            pe.wait_ge(const_ready, 1)
            pe.matmul(ps[:, 0, 0:D], w("a1_wv"), w("a1_wo_t"), start=True, stop=True)
            pe.matmul(ps[:, 0, D:2 * D], bv_wide[:, :], w("a1_wo_t"), start=True, stop=True).then_inc(fused, 1)
            pe.wait_ge(const_ready, 2)

            def mix(t, b, heads=range(HALF)):
                rows = slice(b * S, (b + 1) * S)
                for h in heads:
                    for half in range(2):
                        mm = pe.matmul(mix_ps[b][half * S:(half + 1) * S, :],
                                       v_heads[rows, half, h * HALF * HD:(h + 1) * HALF * HD],
                                       e[t.m][rows, half * HALF + h, :], start=(h == 0), stop=(h == HALF - 1))
                return mm

            EARLY = HALF // 2
            turned = ((2, x3_ready, x3), (3, x4_ready, x4), (8, x5_ready, x5))

            def step(j):
                for r in range(2):
                    if t := j.tile(7):
                        if r == 1 and not j.tile(4):
                            wait(pe, xkt_ready, before(j, 3))
                        mix(t, r, range(0 if r else EARLY, HALF)).then_inc(mix_done, 1)
                    if t := j.tile(4):
                        pe.wait_ge(qexp_ready, 2 * t.n + r + 1)
                        if r == 0:
                            pe.wait_ge(xkt_ready, t.n + 1)
                            wait(pe, s_read, t.n)
                        mm = pe.matmul(s_ps[:, r, :], xk_t[:, r, :], q_heads[:, r, :, :].rearrange("p h n -> p (h n)"),
                                       start=True, stop=True)
                        if r == 1:
                            mm.then_inc(s_done, 1)
                wait(pe, turned_ready, turned_before(j))
                if t := j.tile(7):
                    pe.wait_ge(mix_ready, 2 * t.n + 2)
                if not j.tile(4):
                    wait(pe, xkt_ready, before(j, 3))
                for k, (lag, ready, src) in enumerate(turned):
                    if t := j.tile(lag):
                        pe.wait_ge(ready, t.n + 1)
                        pe.transpose(turned_ps[k], src[t.m % len(src)][:, :], w("ident")).then_inc(turned_done, 1)
                if isinstance(j.n, int):
                    wait(pe, xk_ready, before(j, 5))
                    wait(pe, v_ready, before(j, 2))
                wait(pe, top_ready, before(j, 8))
                if t := j.tile(5):
                    mm_rows = pe.matmul(xk_ps, ctx_t[t.m][:, :], w("x1_wk"), start=True, stop=True)
                if t := j.tile(2):
                    pe.wait_ge(turned_ready, turned_before(j) + 1)
                    wait(pe, kq_ready, t.n)
                    pe.matmul(k_ps, w("a1_wk_t"), turned_t[:, 0:P], start=True, stop=True)
                    pe.matmul(q_ps, w("a1_wq_t"), turned_t[:, 0:P], start=True, stop=True).then_inc(kq_done, 1)
                if isinstance(j.n, int):
                    wait(pe, attn_added, before(j, 2))
                    wait(pe, xattn_added, before(j, 7))
                wait(pe, ffn_added, before(j, 8))
                if t := j.tile(7):
                    mm = pe.matmul(wo_ps, mix_t[:, :], w("x1_wo"), start=True, stop=True)
                if j.tile(3) or j.tile(8):
                    pe.wait_ge(turned_ready, turned_before(j, 1))
                if isinstance(j.n, int):
                    wait(pe, hid_relu, before(j, 8))
                wait(pe, xq_ready, before(j, 3))
                if t := j.tile(3):
                    for r in range(2):
                        for b in range(PER):
                            mm_side = pe.matmul(xq_ps[b * S:(b + 1) * S, r, :], w("x1_wq")[:, r * S:(r + 1) * S],
                                           turned_t[:, P + b * S:P + (b + 1) * S], start=True, stop=True)
                if t := j.tile(8):
                    mm_side = pe.matmul(hid_ps, w("shared_w1"), turned_t[:, 2 * P:3 * P], start=True, stop=True)
                if j.tile(3) or j.tile(8):
                    mm_side.then_inc(side_done, 1)
                if t := j.tile(2):
                    mm_rows = pe.matmul(v_ps, turned_t[:, 0:P], wvo[:, :], start=True, stop=True)
                if t := j.tile(8):
                    mm_rows = pe.matmul(lg_ps, turned_t[:, 2 * P:3 * P], w("route_w"), start=True, stop=True)
                if t := j.tile(2):
                    pe.wait_ge(kq_ready, t.n + 1)
                    pe.matmul(st_ps, k_t[:, :], q_t[:, :], start=True, stop=True).then_inc(st_done, 1)
                if j.tile(2) or j.tile(5) or j.tile(8):
                    mm_rows.then_inc(rows_done, 1)
                if t := j.tile(3):
                    wait(pe, xkt_ready, t.n)
                    pe.wait_ge(ctx_loaded[t.m], 16 * (t.q + 1))
                    for r in range(2):
                        for b in range(PER):
                            if (t6 := j.tile(6)) and r == b == 1:
                                pe.wait_ge(vexp_ready, t6.n + 1)
                                pe.wait_ge(e_ready, t6.n + 1)
                            mm = pe.matmul(xkt_ps[b * S:(b + 1) * S, r, :], w("x1_wk")[:, r * S:(r + 1) * S],
                                           ctx_t[t.m][:, b * S:(b + 1) * S], start=True, stop=True)
                    mm.then_inc(xkt_done, 1)
                if t := j.tile(6):
                    if not j.tile(3):
                        pe.wait_ge(vexp_ready, t.n + 1)
                        pe.wait_ge(e_ready, t.n + 1)
                    mix(t, 0, range(EARLY))
                if t := j.tile(2):
                    pe.wait_ge(sim_ready, t.n + 1)
                    pe.wait_ge(v_ready, t.n + 1)
                    mm = pe.matmul(z_ps, sim[:, :], v[:, :], start=True, stop=True)
                if t := j.tile(8):
                    pe.wait_ge(hid_ready, t.n + 1)
                    mm = pe.matmul(ffn_ps, hid2[:, :], w("shared_w2")[0:M1, :], start=True, stop=True)
                if j.tile(2) or j.tile(7) or j.tile(8):
                    mm.then_inc(sums_done, 1)

            run_turns(pe, step, LAGS, ahead=2)

        @block.scalar
        def _(act):
            act.wait_ge(const_ready, 2)
            def step(j):
                if t := j.tile(7):
                    act.wait_ge(mix_done, 2 * t.n + 1)
                    wait(act, sums_done, turns(j, 2) - 1)
                    act.activation(mix_t[:, 0:S], mix_ps[0], ACT.Copy).then_inc(mix_ready, 1)
                if t := j.tile(7):
                    act.wait_ge(mix_done, 2 * t.n + 2)
                    act.activation(mix_t[:, S:P], mix_ps[1], ACT.Copy).then_inc(mix_ready, 1)
                if t := j.tile(6):
                    act.wait_ge(sub_ready, t.n + 1)
                    act.activation(e[t.m][:, :, :], e[t.m][:, :, :], ACT.Exp).then_inc(e_ready, 1)
                here = [k for k, lag in enumerate(C_LAGS) if k and j.tile(lag)]
                if j.tile(2):
                    act.wait_ge(turned_done, turned_count(j, C_LAGS) - len(here))
                    act.activation(turned_t[:, 0:P], turned_ps[0], ACT.Copy).then_inc(turned_ready, 1)
                if here:
                    act.wait_ge(turned_done, turned_count(j, C_LAGS))
                    act.activation(turned_t[:, here[0] * P:(here[-1] + 1) * P], ps[:, 3, (here[0] - 1) * P:here[-1] * P],
                                   ACT.Copy).then_inc(turned_ready, 1)
                if t := j.tile(2):
                    act.wait_ge(kq_done, t.n + 1)
                    wait(act, st_done, t.n)
                    act.activation(k_t[:, :], k_ps, ACT.Identity, bias=w("a1_bk"))
                    act.activation(q_t[:, :], q_ps, ACT.Identity, bias=w("a1_bq")).then_inc(kq_ready, 1)
                if t := j.tile(4):
                    act.wait_ge(s_done, t.n + 1)
                    wait(act, mix_done, 2 * (t.n - UNROLL + 1))
                    act.activation(e[t.m][:, :, :].rearrange("p h n -> p (h n)"), s_ps.rearrange("p r n -> p (r n)"),
                                   ACT.Copy).then_inc(s_read, 1)
                if t := j.tile(8):
                    act.wait_ge(side_done, turns(j, 3))
                    act.activation(hid[:, :], hid_ps, ACT.Relu).then_inc(hid_relu, 1)
                if t := j.tile(3):
                    act.wait_ge(side_done, turns(j, 3))
                    wait(act, qexp_ready, 2 * t.n)
                    for r in range(2):
                        last = act.activation(xq_t[:, r, :], xq_ps[:, r, :], ACT.Identity, bias=w("x1_bq")[:, r:r + 1])
                    last.then_inc(xq_ready, 1)
                if t := j.tile(8):
                    act.wait_ge(hid_relu, t.n + 1)
                    wait(act, sums_done, turns(j, 2) - 1)
                    act.activation(hid2[:, :], hid[:, :], ACT.Square).then_inc(hid_ready, 1)
                if t := j.tile(3):
                    act.wait_ge(xkt_done, t.n + 1)
                    wait(act, s_done, t.n)
                    for r in range(2):
                        for b in range(PER):
                            own = slice(b * S, (b + 1) * S)
                            last = act.activation(xk_t[own, r, own], xkt_ps[own, r, :], ACT.Identity,
                                                  bias=w("x1_bk")[own, r:r + 1])
                    last.then_inc(xkt_ready, 1)
                lanes = [k for k, lag in enumerate((1, 2, 7, 8)) if j.tile(lag)]
                if lanes:
                    norm_scalar(act, norm, j.n, lanes[0], lanes[-1] + 1)

            run_turns(act, step, LAGS, ahead=2)

        @block.gpsimd
        def _(pool):
            def step(j):
                if isinstance(j.n, int) and j.n == 2:
                    pool.wait_ge(const_ready, 2)
                if t := j.tile(2):
                    pool.wait_ge(x3_ready, t.n + 1)
                    wait(pool, attn_added, t.n - 1)
                    pool.tensor_tensor(x3_plus[t.m % 2][:, :], x3[t.m % 2][:, :], w("a1_bo"), ALU.add).then_inc(x3p_ready, 1)
                if t := j.tile(0):
                    pool.wait_ge(idx_ready, t.n + 1)
                    wait(pool, x3_added, t.n - 1)
                if t := j.tile(4):
                    pool.wait_ge(x4_ready, t.n + 1)
                    wait(pool, xattn_added, t.n - UNROLL + 1)
                    pool.tensor_tensor(x4_plus[t.m][:, :], x4[t.m][:, :], w("x1_bo"), ALU.add).then_inc(x4p_ready, 1)
                if t := j.tile(3):
                    pool.wait_ge(xq_ready, t.n + 1)
                    wait(pool, s_done, t.n)
                    for r in range(2):
                        pool.tensor_tensor(q_heads[:, r, :, :], spread(xq_t[:, r, :], 1, HALF),
                                           spread(head_scaled[:, :], 2, S), ALU.mult).then_inc(qexp_ready, 1)
                if t := j.tile(5):
                    pool.wait_ge(max_ready, t.n + 1)
                    pool.tensor_tensor(e[t.m][:, :, :], e[t.m][:, :, :], spread(row_max[t.m % 2][:, :], 2, S),
                                       ALU.subtract).then_inc(sub_ready, 1)
                if t := j.tile(0):
                    pool.indirect_dma_start(y[t.m % 2][:, :], None, io.y,
                                            bass.IndirectOffsetOnAxis(ap=idx[t.m % 2][:, 0:1], axis=0)).then_inc(gathered[t.m % 2], 16)
                if t := j.tile(8):
                    pool.wait_ge(top_ready, t.n + 1)
                    pool.tensor_tensor(pick(keep.gap, t), top[t.m][:, 0:1], top[t.m][:, 1:2],
                                       ALU.subtract).then_inc(gap_ready, 1)

            run_turns(pool, step, LAGS, ahead=2)

        @block.vector
        def _(dve):
            chain = Chain(dve, chain_c)
            for n in range(2):
                dve.tensor_copy(idx[n][:, :], keep.rows[:, n:n + 1]).then_inc(idx_ready, 1)
            dve.tensor_copy(bv_wide[:, :], w("a1_bv").broadcast_to([P, P]))
            dve.tensor_scalar(head_scaled[:, :], w("head_of_row"), HD ** -0.5, None, ALU.mult).then_inc(const_ready, 1)
            dve.memset(v_heads[:, :, :], 0.0)
            dve.memset(xk_t[:, :, :], 0.0)
            dve.memset(norm.idle[:, :], 0.0)
            dve.wait_ge(fused, 1)
            dve.tensor_copy(wvo[:, :], ps[:, 0, 0:D])
            chain.link(dve.tensor_copy(bvo[:, :], ps[:, 0, D:2 * D]))
            dve.tensor_copy(norm.idle[:, 0:1], norm.idle[:, 1:2]).then_inc(const_ready, 1)

            def largest(t, half):
                own = slice(half * HALF, (half + 1) * HALF)
                return dve.tensor_reduce(row_max[t.m % 2][:, own], e[t.m][:, own, :], axis=AX.X, op=ALU.max)

            def step(j):
                if (t := j.tile(0)) and not (isinstance(t.n, int) and t.n < 2):
                    wait(dve, gathered[t.m % 2], 32 * t.q + 16 * (t.m // 2))
                    dve.tensor_copy(idx[t.m % 2][:, :], pick(keep.rows, t)).then_inc(idx_ready, 1)
                if t := j.tile(6):
                    dve.wait_ge(e_ready, t.n + 1)
                    dve.wait_ge(xk_ready, t.n + 1)
                    wait(dve, mix_done, 2 * t.n)
                    summed = chain.mark(dve.tensor_reduce(rsum[:, :], e[t.m][:, :, :], axis=AX.X, op=ALU.add))
                if t := j.tile(6):
                    chain.wait(summed)
                    inverted = chain.mark(dve.reciprocal(rden[:, :], rsum[:, :]))
                if t := j.tile(6):
                    chain.wait(inverted)
                    dve.tensor_tensor(v_heads[:, :, :].rearrange("p g (h n) -> p g h n", h=HALF)[:, :, :, 0:HD],
                                      xk[t.m % 2][:, :].rearrange("p (g h n) -> p g h n", g=2, h=HALF),
                                      spread(rden[:, :].rearrange("p (g h) -> p g h", g=2), 3, HD),
                                      ALU.mult).then_inc(vexp_ready, 1)
                if t := j.tile(5):
                    largest(t, 1).then_inc(max_ready, 1)
                if t := j.tile(2):
                    wait(dve, sums_done, before(j, 2))
                    dve.wait_ge(st_done, t.n + 1)
                    dve.tensor_tensor(sim[:, :], st_ps, w("decay"), ALU.mult).then_inc(sim_ready, 1)
                if j.tile(2) or j.tile(5) or j.tile(8):
                    dve.wait_ge(rows_done, turns(j, 2))
                    if t := j.tile(8):
                        wait(dve, gap_ready, t.n - 1)
                if t := j.tile(2):
                    wait(dve, sums_done, before(j, 2))
                    dve.tensor_tensor(v[:, :], v_ps, bvo[:, :], ALU.add).then_inc(v_ready, 1)
                if t := j.tile(5):
                    wait(dve, vexp_ready, t.n - 1)
                    dve.tensor_tensor(xk[t.m % 2][:, :], xk_ps, w("x1_bk_row"), ALU.add).then_inc(xk_ready, 1)
                if t := j.tile(8):
                    dve.max(out=top[t.m][:, :], in_=lg_ps).then_inc(top_ready, 1)
                lanes = []
                if t := j.tile(1):
                    dve.wait_ge(x_loaded[t.m % 2], 32 * t.q + 16 * (t.m // 2 + 1))
                    dve.wait_ge(gathered[t.m % 2], 32 * t.q + 16 * (t.m // 2 + 1))
                    dve.scalar_tensor_tensor(norm.sum[0][:, :], y[t.m % 2][:, :], pick(keep.prob, t), x2[t.m % 2][:, :],
                                             ALU.mult, ALU.add).then_inc(x3_added, 1)
                    dve.wait_ge(x3_added, t.n + 1)
                    dve.bn_stats(norm.stats[:, 0, :], norm.sum[0][:, :])
                    lanes.append((0, x3[t.m % 2][:, :], x3_ready, lambda t=t: wait(dve, x3p_ready, t.n - 1)))
                if j.tile(2) or j.tile(7) or j.tile(8):
                    dve.wait_ge(sums_done, turns(j, 2))
                if t := j.tile(2):
                    dve.wait_ge(x3p_ready, t.n + 1)
                    dve.tensor_tensor(norm.sum[1][:, :], z_ps, x3_plus[t.m % 2][:, :], ALU.add).then_inc(attn_added, 1)
                    lanes.append((1, x4[t.m][:, :], x4_ready, lambda t=t: wait(dve, x4p_ready, t.n - UNROLL + 1)))
                if t := j.tile(7):
                    dve.wait_ge(x4p_ready, t.n + 1)
                    dve.tensor_tensor(norm.sum[2][:, :], wo_ps, x4_plus[t.m][:, :], ALU.add).then_inc(xattn_added, 1)
                    lanes.append((2, x5[t.m % 2][:, :], x5_ready,
                                  lambda t=t: wait(dve, x5_stored[t.m % 2], 32 * t.q + 16 * (t.m // 2))))
                if t := j.tile(8):
                    dve.wait_ge(x5_ready, t.n + 1)
                    wait(dve, out_ready, t.n)
                    dve.tensor_tensor(norm.sum[3][:, :], ffn_ps, x5[t.m % 2][:, :], ALU.add).then_inc(ffn_added, 1)
                    lanes.append((3, result[t.m % 2][:, :], out_ready,
                                  lambda t=t: wait(dve, out_stored[t.m % 2], 32 * t.q + 16 * (t.m // 2))))
                meanwhile = lambda: None
                if t := j.tile(4):
                    dve.wait_ge(s_read, t.n + 1)
                    wait(dve, sub_ready, t.n - 1)
                    meanwhile = lambda t=t: largest(t, 0)
                if lanes:
                    summed = {k: (sem, j.tile(lag).n + 1) for k, (lag, sem) in
                              enumerate(((2, attn_added), (7, xattn_added), (8, ffn_added)), 1) if j.tile(lag)}
                    norm_vector(dve, chain, norm, j.n, lanes, counted=(0,), summed=summed, meanwhile=meanwhile)

            run_turns(dve, step, LAGS, chain, LINKS_C, ahead=2)


GAP = 16.0
LINKS_D = 17


def layer1_routed(nc, io, keep):
    with ExitStack() as ctx:
        new = lambda name, shape, dt=F32: ctx.enter_context(nc.sbuf_tensor(name, shape, dt))
        sems = lambda name: ctx.enter_context(nc.semaphore(name))
        w = lambda name: WEIGHTS.cols(keep.weights, name)
        ps = ctx.enter_context(nc.psum_tensor("ps_d", [P, 8, 512], F32))
        pairs = E1 // 2

        gap_max = new("gap_max", [P, 1])
        all_max = new("all_max", [1, 1])
        flag = new("flag", [1, 1], I32)
        w1, w2 = new("w1_d", [P, E1 * M1]), new("w2_d", [P, pairs, D])
        x5, x5_t = new("x5_d", [P, D]), new("x5_td", [P, P])
        hid, hid2 = new("hid_d", [P, pairs, P]), new("hid2_d", [P, pairs, P])
        own, own2 = new("own_d", [M1, P]), new("own2_d", [M1, P])
        lg, top, top_at, top_f = new("lg_d", [P, E1]), new("top_d", [P, 8]), new("top_at_d", [P, 8], U32), new("top_fd", [P, 1])
        gap, other = new("gap_d", [P, 1]), new("other_d", [P, 1])
        kept, chosen = new("kept_d", [P, 1]), new("chosen_d", [P, E1])
        result = new("result_d", [P, D])
        norm = Norm(new, sems, "n2", 1)

        (gap_ready, max_turned, flag_ready, loaded, turned_done, turned_ready, hid_done, hid_ready, squared, gap2_ready,
         exp_ready, y_done, added, out_ready, moved, chain_d) = (sems(n + "_d") for n in (
             "gap_ready", "max_turned", "flag_ready", "loaded", "turned_done", "turned_ready", "hid_done",
             "hid_ready", "squared", "gap2_ready", "exp_ready", "y_done", "added", "out_ready", "moved", "chain"))
        hid_ps = ps[:, 1, :]
        own_ps = ps[0:M1, 2, 0:P]
        lg_ps = ps[:, 3, 0:E1]
        shared_ps = ps[:, 6, 0:D]

        block = ctx.enter_context(nc.Block())

        def needed(eng):
            eng.wait_ge(flag_ready, 1)
            return eng.value_load(flag[0:1, 0:1], min_val=0, max_val=1) > 0

        @block.sync
        def _(sp):
            with sp.If(needed(sp)):
                sp.dma_start(w1[:, :], io.routed_w1).then_inc(moved, 16)
                sp.dma_start(w2[:, :, :].rearrange("p c n -> p (c n)"), io.routed_w2).then_inc(moved, 16)
                with sp.Fori(0, TILES) as i:
                    sp.wait_ge(moved, i * 16 + 32)
                    sp.dma_start(x5[:, :], plane(io.x5, i)).then_inc(loaded, 16)
                    sp.wait_ge(out_ready, i + 1)
                    sp.dma_start(plane(io.out, i), result[:, :]).then_inc(moved, 16)
                sp.wait_ge(moved, 16 * TILES + 32)

        @block.tensor
        def _(pe):
            pe.wait_ge(gap_ready, 1)
            pe.transpose(ps[0:1, 7, 0:P], gap_max[:, :], w("ident")).then_inc(max_turned, 1)
            with pe.If(needed(pe)):
                with pe.Fori(0, TILES) as i:
                    pe.wait_ge(loaded, i * 16 + 16)
                    pe.transpose(ps[:, 0, 0:P], x5[:, :], w("ident")).then_inc(turned_done, 1)
                    pe.wait_ge(turned_ready, i + 1)
                    pe.matmul(lg_ps, x5_t[:, :], w("route_w"), start=True, stop=True)
                    for c in range(pairs):
                        pe.matmul(hid_ps[:, c * P:(c + 1) * P], w1[:, c * P:(c + 1) * P], x5_t[:, :], start=True, stop=True)
                    pe.matmul(own_ps, w("shared_w1"), x5_t[:, :], start=True, stop=True).then_inc(hid_done, 1)
                    pe.wait_ge(squared, i + 1)
                    pe.matmul(shared_ps, own2[:, :], w("shared_w2")[0:M1, :], start=True, stop=True)
                    for c in range(pairs):
                        for k in range(2):
                            rows = slice(k * M1, (k + 1) * M1)
                            mm = pe.matmul(ps[:, 4 + k, c * D:(c + 1) * D], hid2[rows, c, :], w2[rows, c, :], start=True, stop=True)
                    mm.then_inc(y_done, 1)

        @block.scalar
        def _(act):
            with act.If(needed(act)):
                with act.Fori(0, TILES) as i:
                    act.wait_ge(turned_done, i + 1)
                    act.activation(x5_t[:, :], ps[:, 0, 0:P], ACT.Copy).then_inc(turned_ready, 1)
                    act.wait_ge(hid_done, i + 1)
                    act.activation(hid[:, :, :].rearrange("p c n -> p (c n)"), hid_ps, ACT.Relu)
                    act.activation(own[:, :], own_ps, ACT.Relu).then_inc(hid_ready, 1)
                    act.wait_ge(gap2_ready, i + 1)
                    act.activation(other[:, :], gap[:, :], ACT.Exp).then_inc(exp_ready, 1)
                    norm_scalar(act, norm, i + 1, 0, 1)

        @block.vector
        def _(dve):
            chain = Chain(dve, chain_d)
            chain.link(dve.memset(norm.idle[:, :], 0.0))
            dve.tensor_reduce(gap_max[:, :], keep.gap[:, :], axis=AX.X, op=ALU.max).then_inc(gap_ready, 1)
            dve.wait_ge(max_turned, 1)
            chain.link(dve.tensor_reduce(all_max[:, :], ps[0:1, 7, 0:P], axis=AX.X, op=ALU.max))
            dve.tensor_scalar(flag[:, :], all_max[:, :], GAP, None, ALU.is_gt).then_inc(flag_ready, 1)
            with dve.If(needed(dve)):
                before = chain.count
                with dve.Fori(0, TILES) as i:
                    chain.turn = (i, LINKS_D, 0)
                    dve.wait_ge(hid_done, i + 1)
                    chain.link(dve.tensor_copy(lg[:, :], lg_ps))
                    dve.tensor_copy(norm.idle[:, 0:1], norm.idle[:, 1:2])
                    chain.link(dve.max(out=top[:, :], in_=lg[:, :]))
                    dve.tensor_tensor(gap[:, :], top[:, 1:2], top[:, 0:1], ALU.subtract).then_inc(gap2_ready, 1)
                    chain.link(dve.max_index(out=top_at[:, :], in_max=top[:, :], in_values=lg[:, :]))
                    dve.tensor_copy(top_f[:, :], top_at[:, 0:1])
                    dve.wait_ge(exp_ready, i + 1)
                    dve.tensor_scalar(kept[:, :], other[:, :], 1.0, 1.0, ALU.add, ALU.is_le)
                    chain.link(dve.tensor_copy(norm.idle[:, 0:1], norm.idle[:, 1:2]))
                    dve.tensor_scalar(chosen[:, :], w("expert_no"), top_f[:, 0:1], kept[:, 0:1], ALU.is_equal, ALU.mult)
                    dve.wait_ge(hid_ready, i + 1)
                    dve.tensor_tensor(hid2[:, :, :], hid[:, :, :], hid[:, :, :], ALU.mult)
                    dve.tensor_tensor(own2[:, :], own[:, :], own[:, :], ALU.mult).then_inc(squared, 1)
                    dve.wait_ge(y_done, i + 1)
                    dve.wait_ge(loaded, i * 16 + 16)
                    dve.tensor_tensor(norm.sum[0][:, :], shared_ps, x5[:, :], ALU.add).then_inc(added, 1)
                    dve.wait_ge(added, i + 1)
                    for k in range(E1):
                        chain.link(dve.scalar_tensor_tensor(norm.sum[0][:, :], ps[:, 4 + k % 2, k // 2 * D:(k // 2 + 1) * D],
                                                            chosen[:, k:k + 1], norm.sum[0][:, :], ALU.mult, ALU.add))
                    norm_vector(dve, chain, norm, i + 1, [(0, result[:, :], out_ready, lambda: None)])
                assert chain.count == before + LINKS_D, chain.count - before


def lay_out(inputs):
    f = {k: np.asarray(v) for k, v in inputs.items()}
    row = lambda a: np.broadcast_to(a.reshape(1, -1), (P, a.size))
    col = lambda a: a.reshape(P, 1)
    head_major = lambda a: a.transpose(1, 0, 2).reshape(P, -1)
    halves = lambda a: np.tile(a.reshape(2, S).T, (PER, 1))
    p, s, c = np.arange(P), np.arange(S), HALF // 2
    const = {
        "ident": np.eye(P), "causal": (s[None] >= p[:, None] % S) / S,
        "head_of_row": p[:, None] % S // HD == np.arange(HALF),
        "expert_no": np.broadcast_to(np.arange(E0), (P, E0)), "region": np.broadcast_to(np.arange(E0) * REGION, (P, E0)),
        "before": p[:, None] < p[None],
        "tile_rows": np.broadcast_to(np.arange(TILES) * P, (P, TILES)), "slot_no": np.broadcast_to(np.arange(SLOTS), (P, SLOTS)),
        "ones_at": (np.arange(HALF)[None, None] == 2 * np.arange(c)[None, :, None] + (p // S)[:, None, None]).reshape(P, -1),
        "decay": np.where((p[:, None] < p[None]) & (p[:, None] // S == p[None] // S),
                          0.01 * 0.99 ** np.maximum(p[None] - p[:, None] - 1, 0).astype(np.float64), 0.0),
    }
    kv = f["L0_xattn_W_kv"].reshape(D, XH, 2, HD)
    b_kv = f["L0_xattn_b_kv"].reshape(XH, 2, HD)
    w2s = np.zeros((P, D), np.float32)
    w2s[:M1] = f["L1_ffn_Ws2"]
    parts = {
        "wq_heads": head_major(f["L0_attn_Wq"]), "wk_heads": head_major(f["L0_attn_Wk"]),
        "wv_t": f["L0_attn_Wv"].transpose(2, 0, 1).reshape(D, -1),
        "x0_wk": kv[:, :, 0].reshape(D, D), "x0_wv": kv[:, :, 1].reshape(D, D), "x0_wq": f["L0_xattn_W_q"],
        "x0_wo": f["L0_xattn_W_o"], "x0_bk": col(b_kv[:, 0]), "x0_bq": col(f["L0_xattn_b_q"]),
        "x0_bv": row(np.tile(b_kv[:, 1].reshape(-1), PER)), "x0_bo": row(f["L0_xattn_b_o"]),
        "gate_w": f["L0_ffn_w_gate"], "gate_b": row(f["L0_ffn_b_gate"]),
        "a1_wk_t": f["L1_attn_Wk"].T, "a1_wq_t": f["L1_attn_Wq"].T, "a1_wv": f["L1_attn_Wv"], "a1_wo_t": f["L1_attn_Wo"].T,
        "a1_bk": col(f["L1_attn_bk"]), "a1_bq": col(f["L1_attn_bq"]), "a1_bv": col(f["L1_attn_bv"]),
        "a1_bo": row(f["L1_attn_bo"]),
        "x1_wq": f["L1_xattn_Wq"], "x1_wk": f["L1_xattn_Wk"], "x1_wo": f["L1_xattn_Wo"], "x1_bq": halves(f["L1_xattn_bq"]),
        "x1_bk": halves(f["L1_xattn_bk"]), "x1_bk_row": row(f["L1_xattn_bk"]), "x1_bo": row(f["L1_xattn_bo"]),
        "shared_w1": f["L1_ffn_Ws1"], "shared_w2": w2s, "route_w": f["L1_ffn_Wr"],
    }
    blob = lambda b: np.concatenate([np.asarray({**parts, **const}[n], np.float32).reshape(P, -1) for n in b.at], axis=1)
    ctx = f["ctx_1024"].reshape(TILES, PER, S, D).transpose(0, 3, 1, 2)
    tokens = f["x"].reshape(TILES, P, D)
    return {
        "first": blob(FIRST), "weights": blob(WEIGHTS), "x": tokens, "x_t": np.ascontiguousarray(tokens.transpose(0, 2, 1)),
        "ctx_t": np.ascontiguousarray(np.broadcast_to(ctx[:, :, :, None], (TILES, D, PER, 2, S))).reshape(TILES, D, -1),
        "ctx_p": np.ascontiguousarray(ctx).reshape(TILES, D, P),
        "mask": np.ascontiguousarray(f["mask_BxSxS2_ik0"].reshape(TILES, P, S).transpose(1, 0, 2)),
        "routed_w1": np.ascontiguousarray(f["L1_ffn_W1"].transpose(1, 0, 2)).reshape(D, -1),
        "routed_w2": np.ascontiguousarray(f["L1_ffn_W2"].reshape(E1 // 2, P, D).transpose(1, 0, 2)).reshape(P, -1),
        "w1": np.ascontiguousarray(f["L0_ffn_W1"].transpose(1, 0, 2)),
        "w2": np.ascontiguousarray(f["L0_ffn_W2"].reshape(E0, CH, P, D).transpose(2, 0, 1, 3)),
        "b1": np.ascontiguousarray(np.broadcast_to(f["L0_ffn_b1"][None], (P, E0, M0))),
        "b2": np.ascontiguousarray(np.broadcast_to(f["L0_ffn_b2"][None], (P, E0, D))),
    }


def build(nc, io):
    with ExitStack() as ctx:
        new = lambda name, shape, dt=F32: ctx.enter_context(nc.sbuf_tensor(name, shape, dt))
        keep = Kept()
        keep.weights = new("weights", [P, WEIGHTS.width])
        keep.rows = new("rows", [P, TILES], I32)
        keep.logits = new("logits", [P, TILES, E0])
        keep.base = new("base", [P, E0])
        keep.prob = new("prob", [P, TILES])
        keep.gap = new("gap", [P, TILES])
        keep.ffn_loaded = ctx.enter_context(nc.semaphore("ffn_loaded"))
        with ExitStack() as experts:
            own = lambda name, shape: experts.enter_context(nc.sbuf_tensor(name, shape, F32))
            keep.w1, keep.w2 = own("w1", [P, E0, M0]), own("w2", [P, E0, CH, D])
            keep.b1, keep.b2 = own("b1", [P, E0, M0]), own("b2", [P, E0, D])
            layer0_attention(nc, io, keep)
            layer0_experts(nc, io, keep)
        layer1(nc, io, keep)
        layer1_routed(nc, io, keep)


def kernel(**inputs):
    import concourse.bacc as _bacc
    from concourse.bass_utils import run_bass_kernel_spmd as _run

    nc = _bacc.Bacc("TRN2", target_bir_lowering=False, num_devices=1)
    laid = lay_out(inputs)
    io = Arrays()
    put = vars(io)
    for name, a in laid.items():
        put[name] = nc.dram_tensor(f"in_{name}", a.shape, mybir.dt.from_np(a.dtype), kind="ExternalInput").ap()
    for name, shape in (("x2", (TILES, P, D)), ("sorted", (E0 * REGION + (SLOTS - TILES) * P, D)),
                        ("y", (SLOTS * P, D)), ("x5", (TILES, P, D))):
        put[name] = nc.dram_tensor(f"mid_{name}", shape, F32, kind="Internal").ap()
    put["out"] = nc.dram_tensor("out_0", (TILES, P, D), F32, kind="ExternalOutput").ap()
    build(nc, io)
    r = _run(nc, [{f"in_{name}": a for name, a in laid.items()}], core_ids=[0])
    return r.results[0]["out_0"].reshape(B, S, D)
```
